# Optimizing a Trainium2 kernel written in Bass

```python
import numpy as np
import jax
import jax.numpy as jnp

def _softmax(x, axis=-1):
    return jax.nn.softmax(x, axis=axis)

def _gelu(x):
    return jax.nn.gelu(x, approximate=True)

def _silu(x):
    return jax.nn.silu(x)

def _sigmoid(x):
    return jax.nn.sigmoid(x)

def _layernorm(x, axis=-1, eps=1e-05):
    m = jnp.mean(x, axis=axis, keepdims=True)
    v = jnp.var(x, axis=axis, keepdims=True)
    return (x - m) / jnp.sqrt(v + eps)

def _scatter_add(tgt, idx, src, axis=0):
    return tgt.at[idx].add(src)

def _segment_sum(src, seg, n):
    return jax.ops.segment_sum(src, seg, n)
kernel_name = 'mk_adaln_d1_jaxref_r8_bc00a9'

def setup_inputs(seed: int=0):
    np.random.seed(seed)
    _w = jnp.asarray

    def _L0_attn_setup():
        import jax, jax.numpy as jnp
        import numpy as np
        D_MODEL = 128
        N_HEADS = 16
        HEAD_DIM = D_MODEL // N_HEADS
        MAX_REL = 128
        B, S = (8, 128)
        key = jax.random.key(seed)
        ks = jax.random.split(key, 12)
        sc = 1.0 / np.sqrt(D_MODEL)
        return {'hidden_states': jax.random.normal(ks[0], (B, S, D_MODEL), jnp.float32), 'Wq': jax.random.normal(ks[1], (D_MODEL, D_MODEL), jnp.float32) * sc, 'bq': jnp.zeros((D_MODEL,), jnp.float32), 'Wk': jax.random.normal(ks[2], (D_MODEL, D_MODEL), jnp.float32) * sc, 'bk': jnp.zeros((D_MODEL,), jnp.float32), 'Wv': jax.random.normal(ks[3], (D_MODEL, D_MODEL), jnp.float32) * sc, 'bv': jnp.zeros((D_MODEL,), jnp.float32), 'Wo': jax.random.normal(ks[4], (D_MODEL, D_MODEL), jnp.float32) * sc, 'bo': jnp.zeros((D_MODEL,), jnp.float32), 'rel_emb': jax.random.normal(ks[5], (2 * MAX_REL + 1, HEAD_DIM), jnp.float32) * 0.02, 'M': jax.random.uniform(ks[6], (N_HEADS, HEAD_DIM, HEAD_DIM), jnp.float32), 'z': jax.random.uniform(ks[7], (N_HEADS, HEAD_DIM), jnp.float32), 'gate_alpha': jnp.float32(0.5)}
    _L0_attn_in = _L0_attn_setup()

    def _L0_ffn_setup():
        import jax, jax.numpy as jnp
        import numpy as np
        E = 32
        H = 128
        I = 64
        G = 8
        TKG = 4
        TOPK = 8
        NSH = 2
        SCALE = 2.5
        key = jax.random.key(seed)
        ks = jax.random.split(key, 10)
        s = 0.02
        return {'hidden_states': jax.random.normal(ks[0], (2, 128, H), jnp.float32), 'gate_w': jax.random.normal(ks[1], (E, H), jnp.float32) * s, 'gate_bias': jax.random.normal(ks[2], (E,), jnp.float32) * s, 'w_gate': jax.random.normal(ks[3], (E, I, H), jnp.float32) * s, 'w_up': jax.random.normal(ks[4], (E, I, H), jnp.float32) * s, 'w_down': jax.random.normal(ks[5], (E, H, I), jnp.float32) * s, 'sh_gate': jax.random.normal(ks[6], (I * NSH, H), jnp.float32) * s, 'sh_up': jax.random.normal(ks[7], (I * NSH, H), jnp.float32) * s, 'sh_down': jax.random.normal(ks[8], (H, I * NSH), jnp.float32) * s}
    _L0_ffn_in = _L0_ffn_setup()
    _L0_c = _w((lambda *s: np.random.randn(*s).astype(np.float32) * 0.05)(8, 128))
    _L0_wmod = _w((lambda *s: np.random.randn(*s).astype(np.float32) * 0.05)(128, 6 * 128) * 128 ** (-0.5))
    _d = {'L0_attn_hidden_states': _L0_attn_in['hidden_states'], 'L0_attn_Wq': _L0_attn_in['Wq'], 'L0_attn_bq': _L0_attn_in['bq'], 'L0_attn_Wk': _L0_attn_in['Wk'], 'L0_attn_bk': _L0_attn_in['bk'], 'L0_attn_Wv': _L0_attn_in['Wv'], 'L0_attn_bv': _L0_attn_in['bv'], 'L0_attn_Wo': _L0_attn_in['Wo'], 'L0_attn_bo': _L0_attn_in['bo'], 'L0_attn_rel_emb': _L0_attn_in['rel_emb'], 'L0_attn_M': _L0_attn_in['M'], 'L0_attn_z': _L0_attn_in['z'], 'L0_attn_gate_alpha': _L0_attn_in['gate_alpha'], 'L0_ffn_gate_w': _L0_ffn_in['gate_w'], 'L0_ffn_gate_bias': _L0_ffn_in['gate_bias'], 'L0_ffn_w_gate': _L0_ffn_in['w_gate'], 'L0_ffn_w_up': _L0_ffn_in['w_up'], 'L0_ffn_w_down': _L0_ffn_in['w_down'], 'L0_ffn_sh_gate': _L0_ffn_in['sh_gate'], 'L0_ffn_sh_up': _L0_ffn_in['sh_up'], 'L0_ffn_sh_down': _L0_ffn_in['sh_down'], 'L0_c': _L0_c, 'L0_wmod': _L0_wmod}
    _x0 = _d['L0_attn_hidden_states']
    _d['L0_attn_hidden_states'] = jax.random.normal(jax.random.fold_in(jax.random.key(seed), 1), (8, 512, 128), dtype=_x0.dtype)
    del _x0
    return _d

def reference(L0_attn_hidden_states, L0_attn_Wq, L0_attn_bq, L0_attn_Wk, L0_attn_bk, L0_attn_Wv, L0_attn_bv, L0_attn_Wo, L0_attn_bo, L0_attn_rel_emb, L0_attn_M, L0_attn_z, L0_attn_gate_alpha, L0_ffn_gate_w, L0_ffn_gate_bias, L0_ffn_w_gate, L0_ffn_w_up, L0_ffn_w_down, L0_ffn_sh_gate, L0_ffn_sh_up, L0_ffn_sh_down, L0_c, L0_wmod):

    def _L0_attn_ref(hidden_states, Wq, bq, Wk, bk, Wv, bv, Wo, bo, rel_emb, M, z, gate_alpha):
        import jax, jax.numpy as jnp
        import numpy as np
        D_MODEL = 128
        N_HEADS = 16
        HEAD_DIM = D_MODEL // N_HEADS
        MAX_REL = 128
        B, S = (8, 128)
        b, s, _ = hidden_states.shape

        def proj(W, bias):
            y = hidden_states @ W.T + bias
            return y.reshape(b, s, N_HEADS, HEAD_DIM).transpose(0, 2, 1, 3)
        q = proj(Wq, bq)
        k = proj(Wk, bk)
        v = proj(Wv, bv)
        dist = jnp.arange(s)[:, None] - jnp.arange(s)[None, :]
        dist = jnp.clip(dist, -MAX_REL, MAX_REL) + MAX_REL
        rel_pos = rel_emb[dist]
        scores = jnp.einsum('bhqd,bhkd->bhqk', q, k)
        scores = scores + jnp.einsum('bhqd,qkd->bhqk', q, rel_pos)
        scores = scores / np.sqrt(HEAD_DIM).astype(np.float32)
        attn = jax.nn.softmax(scores, axis=-1)
        local_ctx = jnp.einsum('bhqk,bhkd->bhqd', attn, v)
        sigma_q = jax.nn.elu(q) + 1.0
        num = jnp.einsum('bhqk,hkv->bhqv', sigma_q, M)
        den = jnp.einsum('bhqk,hk->bhq', sigma_q, z) + 1e-06
        global_attn = num / den[..., None]
        gate = jax.nn.sigmoid(gate_alpha)
        combined = gate * local_ctx + (1.0 - gate) * global_attn
        out = combined.transpose(0, 2, 1, 3).reshape(b, s, D_MODEL)
        return out @ Wo.T + bo

    def _L0_ffn_ref(hidden_states, gate_w, gate_bias, w_gate, w_up, w_down, sh_gate, sh_up, sh_down):
        import jax, jax.numpy as jnp
        import numpy as np
        E = 32
        H = 128
        I = 64
        G = 8
        TKG = 4
        TOPK = 8
        NSH = 2
        SCALE = 2.5
        B, S, Hd = hidden_states.shape
        h = hidden_states.reshape(-1, Hd)
        logits = h.astype(jnp.float32) @ gate_w.T
        scores = jax.nn.sigmoid(logits)
        sc = scores + gate_bias
        grp = sc.reshape(-1, G, E // G)
        group_scores = jax.lax.top_k(grp, 2)[0].sum(-1)
        gidx = jax.lax.top_k(group_scores, TKG)[1]
        gmask = jnp.sum(jax.nn.one_hot(gidx, G, dtype=sc.dtype), axis=1)
        smask = jnp.repeat(gmask, E // G, axis=1)
        masked = jnp.where(smask > 0, sc, jnp.zeros_like(sc))
        tki = jax.lax.top_k(masked, TOPK)[1]
        tkw = jnp.take_along_axis(scores, tki, axis=1)
        tkw = tkw / (tkw.sum(-1, keepdims=True) + 1e-20)
        tkw = tkw * SCALE
        combine = (jax.nn.one_hot(tki, E, dtype=tkw.dtype) * tkw[..., None]).sum(1)
        g = jax.nn.silu(jnp.einsum('th,eih->tei', h, w_gate))
        u = jnp.einsum('th,eih->tei', h, w_up)
        routed = jnp.einsum('tei,ehi->th', g * u * combine[:, :, None], w_down)
        sg = jax.nn.silu(h @ sh_gate.T)
        shared = sg * (h @ sh_up.T) @ sh_down.T
        return (routed + shared).reshape(B, S, Hd)
    x = L0_attn_hidden_states
    mod = (_silu(L0_c) @ L0_wmod).reshape(L0_c.shape[0], 6, 1, -1)
    sa, ca, ga, sb, cb, gb = (mod[:, 0], mod[:, 1], mod[:, 2], mod[:, 3], mod[:, 4], mod[:, 5])
    ga = (2 * (ga >= 0) - 1) * jnp.maximum(jnp.abs(ga), 0.25)
    gb = (2 * (gb >= 0) - 1) * jnp.maximum(jnp.abs(gb), 0.25)
    h = _layernorm(x, axis=-1) * (1 + ca) + sa
    x = x + ga * _L0_attn_ref(h, L0_attn_Wq, L0_attn_bq, L0_attn_Wk, L0_attn_bk, L0_attn_Wv, L0_attn_bv, L0_attn_Wo, L0_attn_bo, L0_attn_rel_emb, L0_attn_M, L0_attn_z, L0_attn_gate_alpha)
    h = _layernorm(x, axis=-1) * (1 + cb) + sb
    x = x + gb * _L0_ffn_ref(h, L0_ffn_gate_w, L0_ffn_gate_bias, L0_ffn_w_gate, L0_ffn_w_up, L0_ffn_w_down, L0_ffn_sh_gate, L0_ffn_sh_up, L0_ffn_sh_down)
    return x

_drawn_inputs = setup_inputs


def setup_inputs(seed=0):
    import zlib

    import numpy as np

    out = dict(_drawn_inputs(seed))
    spreads = {'L0_attn_bq': (0.0, 0.8),
     'L0_attn_bk': (0.0, 0.8),
     'L0_attn_bv': (0.0, 0.556),
     'L0_attn_bo': (0.0, 0.326)}
    factors = {'L0_attn_Wk': 3.298,
     'L0_attn_Wv': 3.072,
     'L0_attn_rel_emb': 8.0,
     'L0_ffn_gate_w': 8.0,
     'L0_ffn_gate_bias': 8.0,
     'L0_ffn_w_gate': 8.0,
     'L0_ffn_w_up': 8.0,
     'L0_ffn_w_down': 8.0,
     'L0_ffn_sh_gate': 8.0,
     'L0_ffn_sh_up': 8.0,
     'L0_ffn_sh_down': 8.0}
    for name, (base, spread) in spreads.items():
        noise = np.random.default_rng([zlib.crc32(name.encode()), seed]).standard_normal(out[name].shape)
        drawn = base * np.exp(spread * noise) if base else spread * noise
        out[name] = jnp.asarray(drawn.astype(out[name].dtype))
    for name, factor in factors.items():
        out[name] = (out[name] * factor).astype(out[name].dtype)
    return out
```

```python
from contextlib import ExitStack

import numpy as np

import concourse.bass as bass
from concourse import mybir

F32 = mybir.dt.float32
BF16 = mybir.dt.bfloat16
ALU = mybir.AluOpType
ACT = mybir.ActivationFunctionType
AX_X = mybir.AxisListType.X

P = 128
B, S, D = 8, 512, 128
H, HD = 16, 8
HP = H // 2
KB = S // P
QG = 32
NG = S // QG
MAX_REL = 128
SLOT = 64
PIECES = [(0, 0), (0, 1), (0, 2), (1, 0), (1, 1), (2, 0)]
MROW = HD * len(PIECES)
TW = 2 * S
E, I, G = 32, 64, 8
TOPG, TOPK = 4, 8
BLK = E * I // P
BIG = 3.0e38
SCORE_SCALE = float(1.0 / np.sqrt(np.float32(HD)))

ONE = 1
PREP_LINKS, OUT_LINKS = 20, 31


def build(nc, a, out):
    ctx = ExitStack()
    with ctx:
        def sb(name, shape, dt=F32):
            return ctx.enter_context(nc.sbuf_tensor(name, shape, dt))

        def sem(name):
            return ctx.enter_context(nc.semaphore(name))

        ident = sb("ident", [P, P])
        identb = sb("identb", [P, P], BF16)
        wq, wk, wv, wo = (sb(n, [P, D]) for n in ("wq", "wk", "wv", "wo"))
        bq, bk = sb("bq", [P, 1]), sb("bk", [P, 1])
        bv, bo = sb("bv", [P, D]), sb("bo", [P, D])
        wmod = sb("wmod", [P, 6 * D])
        mz = sb("mz", [P, D + H])
        gate, one_minus_gate = sb("gate", [P, 1]), sb("one_minus_gate", [P, 1])
        gate_in = sb("gate_in", [P, 1])
        rel_piece = sb("rel_piece", [P, TW], BF16)
        rel = sb("rel", [P, TW], BF16)
        piece_mask = sb("piece_mask", [P, 3])
        w_router = sb("w_router", [P, E])
        b_router = sb("b_router", [P, E])
        wg = sb("wg", [P, BLK + 1, P])
        wu = sb("wu", [P, BLK + 1, P])
        wd = sb("wd", [P, BLK + 1, P])
        sel32 = sb("sel32", [3 * E, E])
        sel = sb("sel", [3 * E, E, I], BF16)

        x = sb("x", [P, KB, D])
        c_col = sb("c_col", [P, 1])
        silu_c = sb("silu_c", [P, 1])
        mod = sb("mod", [P, 6, D])
        mod_mag = sb("mod_mag", [P, 2, D])
        stats = sb("stats", [P, KB, 6])
        mean_var = sb("mean_var", [P, KB, 2])
        std = sb("std", [P, KB])
        rstd = sb("rstd", [P, KB])
        h_nat = sb("h_nat", [P, KB, D])
        h_t = sb("h_t", [P, S])
        q_t, k_t = sb("q_t", [P, S]), sb("k_t", [P, S])
        q_pc, k_pc = sb("q_pc", [P, 3, S], BF16), sb("k_pc", [P, 3, S], BF16)
        q_even, q_odd = sb("q_even", [P, 3, S], BF16), sb("q_odd", [P, 3, S], BF16)
        sigma = sb("sigma", [P, S])
        v_ones = sb("v_ones", [P, KB, H, 32])
        linear = sb("linear", [P, KB, D])
        linear_den = sb("linear_den", [P, KB, H])
        kst = sb("kst", [P, HP, S], BF16)
        qst = sb("qst", [P, HP, 2, S], BF16)
        qrel = sb("qrel", [P, H, S], BF16)
        zrow = sb("zrow", [1, S], BF16)
        key_max = sb("key_max", [P, 2, S], BF16)
        col_max = sb("col_max", [P, KB, NG], BF16)
        max_rows = sb("max_rows", [KB * NG, P], BF16)
        probs = sb("probs", [P, 2, H, S])

        spare = probs[:].rearrange("p a h q -> p (a h q)")
        first_copy = spare[:, 0:2 * S].rearrange("p (a q) -> p a q", a=2)
        run_max = spare[:, 2 * S:6 * S].rearrange("p (a c q) -> p a c q", a=2, c=2)
        silu_g = spare[:, 8 * S:10 * S].rearrange("p (a q) -> p a q", a=2)
        gated = spare[:, 10 * S:12 * S].rearrange("p (a q) -> p a q", a=2)
        inner = spare[:, 12 * S:14 * S].rearrange("p (a q) -> p a q", a=2)
        ctx_t = spare[:, 16 * S:20 * S].rearrange("p (a q) -> p a q", a=4)
        y_t = spare[:, 20 * S:21 * S]
        sigma_e = spare[:, 21 * S:22 * S]
        q_rest, k_rest = spare[:, 22 * S:23 * S], spare[:, 23 * S:24 * S]
        rel32 = spare[:, 0:TW]
        rel_rest = spare[:, TW:2 * TW]
        den_inv = sb("den_inv", [P, KB * H])
        comb = sb("comb", [P, KB, D])
        h_norm = comb
        comb_t = sb("comb_t", [P, S])
        x1 = sb("x1", [P, KB, D])
        h2_t = sb("h2_t", [P, S])
        score = sb("score", [P, KB, E])
        biased = sb("biased", [P, KB, E])
        pair_hi, pair_lo = sb("pair_hi", [P, KB * G, 2]), sb("pair_lo", [P, KB * G, 2])
        top1, top2 = sb("top1", [P, KB * G]), sb("top2", [P, KB * G])
        low_hi = sb("low_hi", [P, KB * G])
        hi_lo = sb("hi_lo", [P, KB * G])
        group_sum = sb("group_sum", [P, KB, G + 4])
        group_top = sb("group_top", [P, KB, 8])
        group_left = sb("group_left", [P, KB, G + 4])
        group_mask = sb("group_mask", [P, KB, G])
        masked = sb("masked", [P, KB, E])
        expert_top = sb("expert_top", [P, KB, 8])
        expert_left = sb("expert_left", [P, KB, E])
        chosen = sb("chosen", [P, KB, E])
        weight = sb("weight", [P, KB, E])
        weight_sum = sb("weight_sum", [P, KB])
        combine = sb("combine", [P, KB, E])
        combine_rest = sb("combine_rest", [P, KB, E])
        combine_pc = sb("combine_pc", [P, KB, 3, E], BF16)
        combine_t = sb("combine_t", [3 * E, S], BF16)
        y = sb("y", [P, KB, D])
        attn = y
        x2 = sb("x2", [P, KB, D])

        ps = ctx.enter_context(nc.psum_tensor("ps", [P, 8, 512], F32))

        k_dram = nc.dram_tensor("k_pieces", [2, HD * H, 3, S], BF16, kind="Internal").ap()[0]
        q_dram = nc.dram_tensor("q_pieces", [3, HD * H, 3, S], BF16, kind="Internal").ap()

        weights_in = sem("weights_in")
        pool_set, vec_set = sem("pool_set"), sem("vec_set")
        rel_chain = sem("rel_chain")
        consts_ready = sem("consts_ready")
        gate_act = sem("gate_act")
        x_in, c_in = sem("x_in"), sem("c_in")
        silu_c_done, mod_done = sem("silu_c_done"), sem("mod_done")
        var_done, std_done = sem("var_done"), sem("std_done")
        h_done, h_turned, h_t_done = sem("h_done"), sem("h_turned"), sem("h_t_done")
        qkv_done, qk_biased, v_done = sem("qkv_done"), sem("qk_biased"), sem("v_done")
        q_pieces_done, k_pieces_done = sem("q_pieces_done"), sem("k_pieces_done")
        parity_done = sem("parity_done")
        pieces_stored, stacks_in = sem("pieces_stored"), sem("stacks_in")
        neg_part_done, neg_exp_done = sem("neg_part_done"), sem("neg_exp_done")
        sigma_done, linear_mm_done, linear_done = sem("sigma_done"), sem("linear_mm_done"), sem("linear_done")
        prep_chain, out_chain = sem("prep_chain"), sem("out_chain")
        scores_a, first_copied, max_steps = sem("scores_a"), sem("first_copied"), sem("max_steps")
        max_turned, group_max_done = sem("max_turned"), sem("group_max_done")
        col_max_turned, max_rows_done, max_in = sem("col_max_turned"), sem("max_rows_done"), sem("max_in")
        scores_b, exps, pv_done = sem("scores_b"), sem("exps"), sem("pv_done")
        ctx_copied_a, ctx_copied_v, ctx_turned = sem("ctx_copied_a"), sem("ctx_copied_v"), sem("ctx_turned")
        comb_done, comb_turned, comb_t_done = sem("comb_done"), sem("comb_turned"), sem("comb_t_done")
        attn_mm_done, residual_done = sem("attn_mm_done"), sem("residual_done")
        var2_done, std2_done, h2_done = sem("var2_done"), sem("std2_done"), sem("h2_done")
        h2_turned, h2_t_done = sem("h2_turned"), sem("h2_t_done")
        logits_done, sigmoid_done = sem("logits_done"), sem("sigmoid_done")
        combine_done, combine_turned, combine_t_done = sem("combine_done"), sem("combine_turned"), sem("combine_t_done")
        gate_mm, up_mm, silu_done, gated_done, inner_done, down_mm = (
            sem("gate_mm"), sem("up_mm"), sem("silu_done"), sem("gated_done"), sem("inner_done"), sem("down_mm"))
        y_t_done, y_turned, y_done, x2_done, stored = (
            sem("y_t_done"), sem("y_turned"), sem("y_done"), sem("x2_done"), sem("stored"))

        carried = [residual_done, silu_c_done, pv_done, pieces_stored, parity_done, mod_done, x2_done, linear_mm_done, comb_done, col_max_turned, max_in, max_steps, gated_done, down_mm, stored]

        bank = [ps[:, n, :] for n in range(8)]

        weight_loads = [
            (ident[:], a["ident"]), (wq[:], a["wq"]), (wk[:], a["wk"]), (wv[:], a["wv"]), (wo[:], a["wo"]),
            (bq[:], a["bq"]), (bk[:], a["bk"]), (bv[:], a["bv"].partition_broadcast(P)),
            (bo[:], a["bo"].partition_broadcast(P)), (wmod[:], a["wmod"]), (mz[:], a["mz"]),
            (gate_in[:], a["gate_alpha"].partition_broadcast(P)), (rel32, a["rel"]),
            (piece_mask[:], a["piece_mask"]), (w_router[:], a["w_router"]),
            (b_router[:], a["b_router"].partition_broadcast(P)),
            (wg[:], a["wg"]), (wu[:], a["wu"]), (wd[:], a["wd"]), (sel32[:], a["sel"]),
        ]
        ALL_WEIGHTS = 16 * len(weight_loads)
        N_STACK = 2 * (3 * len(PIECES) + 1)
        N_MAX = 4 * 4

        def stack_rows(slot, r):
            return slice(SLOT * slot + HD * r, SLOT * slot + HD * (r + 1))

        block = ctx.enter_context(nc.Block())

        @block.sync
        def _(sp):
            for dst, src in weight_loads:
                sp.dma_start(dst, src).then_inc(weights_in, 16)
            sp.wait_ge(pool_set, 5)
            with sp.Fori(0, B) as b:
                sp.wait_ge(residual_done, ONE + b)
                sp.nop(nofuse=True)
                sp.dma_start(x[:], a["x"][bass.ds(b, 1)].rearrange("o (n p) d -> p (o n) d", p=P)).then_inc(x_in, 16)
                sp.wait_ge(silu_c_done, ONE + b)
                sp.nop(nofuse=True)
                sp.dma_start(c_col[:], a["c"][bass.ds(b, 1)].rearrange("o p -> p o")).then_inc(c_in, 16)

                sp.wait_ge(k_pieces_done, b + 1)
                sp.dma_start(k_dram, k_pc[:]).then_inc(pieces_stored, 16)
                sp.wait_ge(q_pieces_done, b + 1)
                sp.dma_start(q_dram[0], q_pc[:]).then_inc(pieces_stored, 16)
                sp.wait_ge(parity_done, ONE + 2 * b + 2)
                sp.dma_start(q_dram[1], q_even[:]).then_inc(pieces_stored, 16)
                sp.dma_start(q_dram[2], q_odd[:]).then_inc(pieces_stored, 16)
                sp.wait_ge(pieces_stored, ONE + 64 * b + 64)
                sp.nop(nofuse=True)
                sp.wait_ge(pv_done, ONE + KB * b)
                for s in range(2):
                    sp.dma_start(qst[SLOT * s + MROW:SLOT * s + MROW + 1, 0:HP, s, :],
                                 zrow[0:1, :].unsqueeze(1).broadcast_to([1, HP, S])).then_inc(stacks_in, 16)
                    for r, (pq, pk) in enumerate(PIECES):
                        rows = stack_rows(s, r)
                        sp.dma_start(kst[rows], k_dram[:, pk, :].rearrange(
                            "(a s d) q -> s d a q", s=2, d=HD)[s]).then_inc(stacks_in, 16)
                        sp.dma_start(qst[rows, :, s, :], q_dram[0][:, pq, :].rearrange(
                            "(a s d) q -> s d a q", s=2, d=HD)[s]).then_inc(stacks_in, 16)
                        sp.dma_start(qrel[rows], q_dram[1 + s][:, pq, :].rearrange(
                            "(h d) q -> d h q", d=HD)).then_inc(stacks_in, 16)

                sp.wait_ge(max_rows_done, b + 1)
                for c in range(4):
                    for s in range(2):
                        for p2 in range(2):
                            sp.dma_start(
                                qst[SLOT * s + MROW:SLOT * s + MROW + 1, 2 * c + p2, s, :],
                                max_rows[NG * c:NG * (c + 1), (2 * p2 + s) * QG:(2 * p2 + s + 1) * QG],
                            ).then_inc(max_in, 16)

                sp.wait_ge(x2_done, ONE + b + 1)
                sp.nop(nofuse=True)
                sp.dma_start(out[bass.ds(b, 1)].rearrange("o (n p) d -> p (o n) d", p=P), x2[:]).then_inc(stored, 16)
            sp.wait_ge(stored, ONE + 16 * B)

        @block.gpsimd
        def _(pool):
            for s in carried:
                pool.sem_inc(s, ONE)
            pool.memset(kst[:], 1.0).then_inc(pool_set, 1)
            pool.memset(qst[:], 0.0).then_inc(pool_set, 1)
            pool.memset(qrel[:], 0.0).then_inc(pool_set, 1)
            pool.memset(zrow[:], 0.0).then_inc(pool_set, 1)
            pool.memset(q_even[:], 0.0).then_inc(pool_set, 1)
            pool.memset(q_odd[:], 0.0).then_inc(pool_set, 1)
            pool.wait_ge(pool_set, 6)
            with pool.Fori(0, B) as b:
                pool.wait_ge(q_pieces_done, b + 1)
                pool.wait_ge(pieces_stored, ONE + 64 * b)
                pool.nop(nofuse=True)
                for parity, dst in enumerate((q_even, q_odd)):
                    pool.tensor_copy(dst[:, :, parity:S:2], q_pc[:, :, parity:S:2]).then_inc(parity_done, 1)

        @block.scalar
        def _(act):
            act.wait_ge(weights_in, ALL_WEIGHTS)
            act.activation(gate[:], gate_in[:], ACT.Sigmoid).then_inc(gate_act, 1)

            def prepare(b):
                act.wait_ge(c_in, 16 * b + 16)
                act.wait_ge(mod_done, ONE + b)
                act.activation(silu_c[:], c_col[:], ACT.Silu).then_inc(silu_c_done, 1)
                act.wait_ge(var_done, b + 1)
                act.activation(std[:], mean_var[:, :, 1], ACT.Sqrt).then_inc(std_done, 1)
                act.wait_ge(h_turned, b + 1)
                act.copy(h_t[:], bank[6]).then_inc(h_t_done, 1)
                act.wait_ge(qkv_done, b + 1)
                act.activation(q_t[:], bank[4], ACT.Identity, bias=bq[:]).then_inc(qk_biased, 1)
                act.activation(k_t[:], bank[5], ACT.Identity, bias=bk[:]).then_inc(qk_biased, 1)
                act.wait_ge(neg_part_done, b + 1)
                act.activation(sigma_e, sigma[:], ACT.Exp).then_inc(neg_exp_done, 1)

            def maxima(b):
                for g in range(NG):
                    act.wait_ge(scores_a, KB * NG * b + KB * g + 1)
                    if g >= 2:
                        act.wait_ge(max_steps, ONE + 3 * NG * b + 3 * (g - 2) + 1)
                    else:
                        act.wait_ge(max_steps, ONE + 3 * NG * b)
                    act.copy(first_copy[:, g % 2, :], bank[0]).then_inc(first_copied, 1)

            def attend(b):
                for kb in range(KB):
                    act.wait_ge(pv_done, ONE + KB * b + max(kb - 1, 0))
                    for g in range(NG):
                        n = kb * NG + g
                        act.wait_ge(scores_b, KB * NG * b + n + 1)
                        act.activation(probs[:, kb % 2, :, QG * g:QG * (g + 1)],
                                       bank[n % 4].rearrange("p (h q) -> p h q", q=QG),
                                       ACT.Exp, scale=SCORE_SCALE).then_inc(exps, 1)

            def output(b):
                act.wait_ge(pv_done, ONE + KB * b + KB)
                for c in range(2):
                    act.copy(ctx_t[:, c, :], bank[4 + c]).then_inc(ctx_copied_a, 1)
                act.wait_ge(comb_turned, b + 1)
                act.copy(comb_t[:], bank[4]).then_inc(comb_t_done, 1)
                act.wait_ge(var2_done, b + 1)
                act.activation(std[:], mean_var[:, :, 1], ACT.Sqrt).then_inc(std2_done, 1)
                act.wait_ge(h2_turned, b + 1)
                act.copy(h2_t[:], bank[6]).then_inc(h2_t_done, 1)
                act.wait_ge(logits_done, b + 1)
                act.activation(score[:], ps[:, 7, 0:KB * E].rearrange("p (n e) -> p n e", e=E),
                               ACT.Sigmoid).then_inc(sigmoid_done, 1)
                act.wait_ge(combine_turned, b + 1)
                act.copy(combine_t[:], bank[4].bitcast(BF16)[0:3 * E, 0:S]).then_inc(combine_t_done, 1)

            def experts(b):
                for n in range(BLK + 1):
                    act.wait_ge(gate_mm, (BLK + 1) * b + n + 1)
                    act.wait_ge(gated_done, ONE + (BLK + 1) * b + max(n - 1, 0))
                    act.activation(silu_g[:, n % 2, :], bank[3 * (n % 2)], ACT.Silu).then_inc(silu_done, 1)
                act.wait_ge(down_mm, ONE + (BLK + 1) * (b + 1))
                act.copy(y_t, bank[7]).then_inc(y_t_done, 1)

            with act.Fori(0, B) as b:
                prepare(b)
                maxima(b)
                attend(b)
                output(b)
                experts(b)

        @block.vector
        def _(dve):
            dve.memset(v_ones[:], 0.0).then_inc(vec_set, 1)
            dve.wait_ge(vec_set, 1)
            dve.memset(v_ones[:, :, :, HD:HD + 1], 1.0).then_inc(vec_set, 1)
            dve.memset(group_sum[:, :, G:G + 4], BIG).then_inc(vec_set, 1)
            dve.wait_ge(weights_in, ALL_WEIGHTS)
            dve.tensor_copy(identb[:], ident[:]).then_inc(consts_ready, 1)
            dve.tensor_copy(sel[:], sel32[:].unsqueeze(2).broadcast_to([3 * E, E, I])).then_inc(consts_ready, 1)
            links = 0

            def rel_link(ins):
                nonlocal links
                links += 1
                ins.then_inc(rel_chain, 1)
                dve.wait_ge(rel_chain, links)

            rel_link(dve.tensor_copy(rel_piece[:], rel32))
            rel_link(dve.tensor_scalar(rel[:], rel_piece[:], piece_mask[:, 0:1], None, ALU.mult))
            for piece in (1, 2):
                rest = rel32 if piece == 1 else rel_rest
                rel_link(dve.tensor_tensor(rel_rest, rest, rel_piece[:], ALU.subtract))
                rel_link(dve.tensor_copy(rel_piece[:], rel_rest))
                rel_link(dve.scalar_tensor_tensor(rel[:], rel_piece[:], piece_mask[:, piece:piece + 1], rel[:],
                                                  ALU.mult, ALU.add))
            dve.wait_ge(gate_act, 1)
            dve.tensor_scalar(one_minus_gate[:], gate[:], -1.0, 1.0, ALU.mult, ALU.add).then_inc(consts_ready, 1)

            def normalise(link, src, which, variance_ready, std_ready, b, chain_no):
                for n in range(KB):
                    last = dve.bn_stats(stats[:, n, :], src[:, n, :])
                link(last)
                dve.nop(nofuse=True)
                for n in range(KB):
                    last = dve.bn_aggr(mean_var[:, n, :], stats[:, n, :])
                link(last)
                dve.tensor_scalar(mean_var[:, :, 1], mean_var[:, :, 1], 1e-5, None, ALU.add).then_inc(variance_ready, 1)
                dve.wait_ge(std_ready, b + 1)
                link(dve.reciprocal(rstd[:], std[:]))
                for n in range(KB):
                    last = dve.tensor_scalar(h_norm[:, n, :], src[:, n, :], mean_var[:, n, 0:1], rstd[:, n:n + 1],
                                             ALU.subtract, ALU.mult)
                link(last)
                return (h_norm[:], mod[:, which + 1, :].unsqueeze(1).broadcast_to([P, KB, D]),
                        mod[:, which, :].unsqueeze(1).broadcast_to([P, KB, D]))

            def prepare(b):
                count = 0

                def link(ins):
                    nonlocal count
                    count += 1
                    ins.then_inc(prep_chain, 1)
                    dve.wait_ge(prep_chain, PREP_LINKS * b + count)

                dve.wait_ge(mod_done, ONE + b + 1)
                dve.wait_ge(x2_done, ONE + b)
                dve.tensor_copy(mod[:, 0:3, :], ps[:, 4, 0:3 * D].rearrange("p (m d) -> p m d", d=D))
                link(dve.tensor_copy(mod[:, 3:6, :], ps[:, 5, 0:3 * D].rearrange("p (m d) -> p m d", d=D)))
                link(dve.tensor_scalar(mod[:, 1:5:3, :], mod[:, 1:5:3, :], 1.0, None, ALU.add))
                link(dve.tensor_scalar(mod_mag[:], mod[:, 2:6:3, :], -1.0, 0.25, ALU.mult, ALU.max))
                link(dve.tensor_tensor(mod_mag[:], mod_mag[:], mod[:, 2:6:3, :], ALU.max))
                link(dve.tensor_scalar(mod[:, 2:6:3, :], mod[:, 2:6:3, :], 0.0, 2.0, ALU.is_ge, ALU.mult))
                link(dve.scalar_tensor_tensor(mod[:, 2:6:3, :], mod[:, 2:6:3, :], 1.0, mod_mag[:],
                                              ALU.subtract, ALU.mult))
                dve.wait_ge(x_in, 16 * b + 16)
                hn, scale, shift = normalise(link, x, 0, var_done, std_done, b, 0)
                link(dve.tensor_tensor(h_nat[:], hn, scale, ALU.mult))
                dve.tensor_tensor(h_nat[:], h_nat[:], shift, ALU.add).then_inc(h_done, 1)

                dve.wait_ge(qkv_done, b + 1)
                dve.wait_ge(pv_done, ONE + KB * b)
                dve.tensor_tensor(v_ones[:, :, :, 0:HD], ps[:, 7, :].rearrange("p (n h d) -> p n h d", h=H, d=HD),
                                  bv[:].rearrange("p (h d) -> p h d", d=HD).unsqueeze(1).broadcast_to([P, KB, H, HD]),
                                  ALU.add).then_inc(v_done, 1)

                dve.wait_ge(pieces_stored, ONE + 64 * b)
                dve.wait_ge(parity_done, ONE + 2 * b)
                for n, (t, rest, pc, done) in enumerate(((q_t, q_rest, q_pc, q_pieces_done),
                                                         (k_t, k_rest, k_pc, k_pieces_done))):
                    dve.wait_ge(qk_biased, 2 * b + 1 + n)
                    link(dve.tensor_copy(pc[:, 0, :], t[:]))
                    link(dve.tensor_tensor(rest, t[:], pc[:, 0, :], ALU.subtract))
                    link(dve.tensor_copy(pc[:, 1, :], rest))
                    dve.tensor_tensor(pc[:, 2, :], rest, pc[:, 1, :], ALU.subtract).then_inc(done, 1)

                dve.wait_ge(linear_mm_done, ONE + b)
                dve.tensor_scalar(sigma[:], q_t[:], 0.0, None, ALU.min).then_inc(neg_part_done, 1)
                dve.wait_ge(neg_exp_done, b + 1)
                dve.scalar_tensor_tensor(sigma[:], q_t[:], 0.0, sigma_e, ALU.max, ALU.add).then_inc(sigma_done, 1)
                dve.wait_ge(linear_mm_done, ONE + b + 1)
                dve.wait_ge(comb_done, ONE + b)
                both = ps[:, 6:8, 0:2 * (D + H)].rearrange("p a (n m) -> p a n m", m=D + H)
                for t in range(2):
                    last = dve.tensor_scalar(linear_den[:, 2 * t:2 * t + 2, :], both[:, t, :, D:D + H], 1e-6, None, ALU.add)
                link(last)
                link(dve.reciprocal(linear_den[:], linear_den[:]))
                link(dve.tensor_scalar(linear_den[:], linear_den[:], one_minus_gate[:], None, ALU.mult))
                for t in range(2):
                    last = dve.tensor_tensor(
                        linear[:, 2 * t:2 * t + 2, :].rearrange("p n (h d) -> p n h d", d=HD),
                        both[:, t, :, 0:D].rearrange("p n (h d) -> p n h d", d=HD),
                        linear_den[:, 2 * t:2 * t + 2, :].unsqueeze(3).broadcast_to([P, 2, H, HD]), ALU.mult)
                last.then_inc(linear_done, 1)
                if count != PREP_LINKS:
                    raise ValueError(f"PREP_LINKS is {count}")

            def maxima(b):
                def group_reduce(g):
                    dve.wait_ge(max_turned, NG * b + g + 1)
                    dve.tensor_reduce(col_max[:, :, g], bank[4 + g % 2].bitcast(BF16)[:, 0:KB * P].rearrange(
                        "p (c k) -> p c k", k=P), AX_X, ALU.max).then_inc(group_max_done, 1)

                dve.wait_ge(col_max_turned, ONE + b)
                for g in range(NG):
                    if g >= 2:
                        dve.wait_ge(max_turned, NG * b + g - 1)
                    for kb in range(1, KB):
                        step = 3 * NG * b + 3 * g + kb
                        src = first_copy[:, g % 2, :] if kb == 1 else run_max[:, g % 2, kb % 2, :]
                        dst = key_max[:, g % 2, :] if kb == KB - 1 else run_max[:, g % 2, (kb + 1) % 2, :]
                        dve.wait_ge(scores_a, KB * NG * b + KB * g + kb + 1)
                        if kb == 1:
                            dve.wait_ge(first_copied, NG * b + g + 1)
                        else:
                            dve.wait_ge(max_steps, ONE + step - 1)
                        dve.tensor_tensor(dst, bank[kb], src, ALU.max).then_inc(max_steps, 1)
                    if g >= 1:
                        group_reduce(g - 1)
                group_reduce(NG - 1)
                dve.wait_ge(col_max_turned, ONE + b + 1)
                dve.wait_ge(max_in, ONE + 16 * N_MAX * b)
                dve.tensor_scalar(max_rows[:], bank[6].bitcast(BF16)[0:KB * NG, 0:P], -1.0, None,
                                  ALU.mult).then_inc(max_rows_done, 1)

            def output(b):
                count = 0

                def link(ins):
                    nonlocal count
                    count += 1
                    ins.then_inc(out_chain, 1)
                    dve.wait_ge(out_chain, OUT_LINKS * b + count)

                dve.wait_ge(pv_done, ONE + KB * b + KB)
                for c in range(2, 4):
                    dve.tensor_copy(ctx_t[:, c, :], bank[4 + c]).then_inc(ctx_copied_v, 1)
                dve.wait_ge(ctx_turned, b + 1)
                local = ps[:, 0:4, :].rearrange("p n (h m) -> p (n h) m", m=32)
                link(dve.reciprocal(den_inv[:], local[:, :, HD]))
                link(dve.tensor_scalar(den_inv[:], den_inv[:], gate[:], None, ALU.mult))
                link(dve.tensor_tensor(comb[:].rearrange("p n (h d) -> p (n h) d", d=HD), local[:, :, 0:HD],
                                       den_inv[:].unsqueeze(2).broadcast_to([P, KB * H, HD]), ALU.mult))
                dve.wait_ge(linear_done, b + 1)
                dve.tensor_tensor(comb[:], comb[:], linear[:], ALU.add).then_inc(comb_done, 1)
                dve.wait_ge(attn_mm_done, b + 1)
                link(dve.tensor_tensor(attn[:], ps[:, 5, :].rearrange("p (n d) -> p n d", d=D),
                                       bo[:].unsqueeze(1).broadcast_to([P, KB, D]), ALU.add))
                link(dve.tensor_tensor(attn[:], attn[:], mod[:, 2, :].unsqueeze(1).broadcast_to([P, KB, D]), ALU.mult))
                dve.tensor_tensor(x1[:], attn[:], x[:], ALU.add).then_inc(residual_done, 1)
                dve.wait_ge(residual_done, ONE + b + 1)
                hn, scale, shift = normalise(link, x1, 3, var2_done, std2_done, b, 1)
                link(dve.tensor_tensor(h_nat[:], hn, scale, ALU.mult))
                dve.tensor_tensor(h_nat[:], h_nat[:], shift, ALU.add).then_inc(h2_done, 1)

                dve.wait_ge(sigmoid_done, b + 1)
                link(dve.tensor_tensor(biased[:], score[:], b_router[:].unsqueeze(1).broadcast_to([P, KB, E]), ALU.add))
                quads = biased[:].rearrange("p n (g j two) -> p (n g) j two", j=2, two=2)
                dve.tensor_tensor(pair_hi[:], quads[:, :, :, 0], quads[:, :, :, 1], ALU.max)
                link(dve.tensor_tensor(pair_lo[:], quads[:, :, :, 0], quads[:, :, :, 1], ALU.min))
                dve.tensor_tensor(top1[:], pair_hi[:, :, 0], pair_hi[:, :, 1], ALU.max)
                dve.tensor_tensor(low_hi[:], pair_hi[:, :, 0], pair_hi[:, :, 1], ALU.min)
                link(dve.tensor_tensor(hi_lo[:], pair_lo[:, :, 0], pair_lo[:, :, 1], ALU.max))
                link(dve.tensor_tensor(top2[:], low_hi[:], hi_lo[:], ALU.max))
                link(dve.tensor_tensor(group_sum[:, :, 0:G], top1[:].rearrange("p (n g) -> p n g", g=G),
                                       top2[:].rearrange("p (n g) -> p n g", g=G), ALU.add))
                dve.nop(nofuse=True)
                for n in range(KB):
                    last = dve.max(group_top[:, n, :], group_sum[:, n, :])
                link(last)
                dve.nop(nofuse=True)
                for n in range(KB):
                    last = dve.match_replace(group_left[:, n, :], group_top[:, n, :], group_sum[:, n, :], -BIG)
                link(last)
                link(dve.tensor_scalar(group_mask[:], group_left[:, :, 0:G], -0.5 * BIG, None, ALU.is_le))
                link(dve.tensor_tensor(masked[:].rearrange("p n (g j) -> p (n g) j", g=G),
                                       biased[:].rearrange("p n (g j) -> p (n g) j", g=G),
                                       group_mask[:].rearrange("p n g -> p (n g)").unsqueeze(2).broadcast_to(
                                           [P, KB * G, E // G]), ALU.mult))
                dve.nop(nofuse=True)
                for n in range(KB):
                    last = dve.max(expert_top[:, n, :], masked[:, n, :])
                link(last)
                dve.nop(nofuse=True)
                for n in range(KB):
                    last = dve.match_replace(expert_left[:, n, :], expert_top[:, n, :], masked[:, n, :], -BIG)
                link(last)
                link(dve.tensor_scalar(chosen[:], expert_left[:], -0.5 * BIG, None, ALU.is_le))
                link(dve.tensor_tensor(weight[:], score[:], chosen[:], ALU.mult))
                link(dve.tensor_reduce(weight_sum[:], weight[:], AX_X, ALU.add))
                link(dve.tensor_scalar(weight_sum[:], weight_sum[:], 1e-20, None, ALU.add))
                link(dve.reciprocal(weight_sum[:], weight_sum[:]))
                link(dve.tensor_tensor(combine[:], weight[:], weight_sum[:].unsqueeze(2).broadcast_to([P, KB, E]),
                                       ALU.mult))
                link(dve.tensor_scalar(combine[:], combine[:], 2.5, None, ALU.mult))
                link(dve.tensor_copy(combine_pc[:, :, 0, :], combine[:]))
                link(dve.tensor_tensor(combine_rest[:], combine[:], combine_pc[:, :, 0, :], ALU.subtract))
                link(dve.tensor_copy(combine_pc[:, :, 1, :], combine_rest[:]))
                dve.tensor_tensor(combine_pc[:, :, 2, :], combine_rest[:], combine_pc[:, :, 1, :],
                                  ALU.subtract).then_inc(combine_done, 1)
                if count != OUT_LINKS:
                    raise ValueError(f"OUT_LINKS is {count}")

            def experts(b):
                for n in range(BLK + 1):
                    e = (BLK + 1) * b + n
                    dve.wait_ge(silu_done, e + 1)
                    dve.wait_ge(up_mm, e + 1)
                    dve.wait_ge(down_mm, ONE + (BLK + 1) * b + max(n - 1, 0))
                    dst = gated if n < BLK else inner
                    dve.tensor_tensor(dst[:, n % 2, :], bank[3 * (n % 2) + 1], silu_g[:, n % 2, :],
                                      ALU.mult).then_inc(gated_done, 1)
                    if n < BLK:
                        dve.wait_ge(gated_done, ONE + e + 1)
                        dve.tensor_tensor(inner[:, n % 2, :], bank[3 * (n % 2) + 2], gated[:, n % 2, :],
                                          ALU.mult).then_inc(inner_done, 1)
                dve.wait_ge(y_turned, b + 1)
                dve.tensor_tensor(y[:], ps[:, 6, :].rearrange("p (n d) -> p n d", d=D),
                                  mod[:, 5, :].unsqueeze(1).broadcast_to([P, KB, D]), ALU.mult).then_inc(y_done, 1)
                dve.wait_ge(y_done, b + 1)
                dve.wait_ge(stored, ONE + 16 * b)
                dve.tensor_tensor(x2[:], y[:], x1[:], ALU.add).then_inc(x2_done, 1)

            with dve.Fori(0, B) as b:
                prepare(b)
                maxima(b)
                output(b)
                experts(b)

        @block.tensor
        def _(pe):
            pe.wait_ge(weights_in, ALL_WEIGHTS)
            pe.wait_ge(consts_ready, 3)
            pe.wait_ge(vec_set, 3)

            def turn(dst, src, identity, parts=KB):
                for n in range(parts):
                    last = pe.transpose(dst(n), src(n), identity)
                return last

            def prepare(b):
                pe.wait_ge(silu_c_done, ONE + b + 1)
                pe.wait_ge(x2_done, ONE + b)
                for half in range(2):
                    last = pe.matmul(ps[:, 4 + half, 0:3 * D], silu_c[:].broadcast_to([P, P]),
                                     wmod[:, 3 * D * half:3 * D * (half + 1)], start=True, stop=True)
                last.then_inc(mod_done, 1)
                pe.wait_ge(h_done, b + 1)
                turn(lambda n: ps[:, 6, P * n:P * (n + 1)], lambda n: h_nat[:, n, :], ident[:]).then_inc(h_turned, 1)
                pe.wait_ge(h_t_done, b + 1)
                pe.matmul(bank[4], wq[:], h_t[:], start=True, stop=True)
                pe.matmul(bank[5], wk[:], h_t[:], start=True, stop=True)
                for n in range(KB):
                    last = pe.matmul(ps[:, 7, P * n:P * (n + 1)], h_t[:, P * n:P * (n + 1)], wv[:],
                                     start=True, stop=True)
                last.then_inc(qkv_done, 1)
                pe.wait_ge(sigma_done, b + 1)
                for n in range(KB):
                    last = pe.matmul(ps[:, 6 + n // 2, (D + H) * (n % 2):(D + H) * (n % 2 + 1)],
                                     sigma[:, P * n:P * (n + 1)], mz[:], start=True, stop=True)
                last.then_inc(linear_mm_done, 1)

            def score_bank(dst, kb, g):
                for hp in range(HP):
                    pe.matmul(dst[:, 2 * QG * hp:2 * QG * (hp + 1)], kst[:, hp, P * kb:P * (kb + 1)],
                              qst[:, hp, :, QG * g:QG * (g + 1)], start=(hp == 0), stop=False,
                              skip_group_check=True)
                by_query = dst.rearrange("p (h q) -> p h q", q=QG)
                for j in range(0, QG, 2):
                    q0 = QG * g + j
                    t0 = P * kb - q0 + S - 1
                    last = pe.matmul(by_query[:, :, j:j + 2], rel[:, t0:t0 + P], qrel[:, :, q0:q0 + 2],
                                     start=False, stop=(j == QG - 2), skip_group_check=True)
                return last

            def maxima(b):
                def turn_maxima(g):
                    pe.wait_ge(max_steps, ONE + 3 * NG * b + 3 * g + 3)
                    if g >= 2:
                        pe.wait_ge(group_max_done, NG * b + g - 1)
                    dst = bank[4 + g % 2].bitcast(BF16)
                    turn(lambda c: dst[:, P * c:P * (c + 1)], lambda c: key_max[:, g % 2, P * c:P * (c + 1)],
                         identb[:]).then_inc(max_turned, 1)

                pe.wait_ge(stacks_in, 16 * N_STACK * (b + 1))
                pe.wait_ge(k_pieces_done, b + 1)
                pe.wait_ge(linear_done, b + 1)
                for g in range(NG):
                    for kb in range(KB):
                        if g >= 1:
                            if kb == 0:
                                pe.wait_ge(first_copied, NG * b + g)
                            else:
                                pe.wait_ge(max_steps, ONE + 3 * NG * b + 3 * (g - 1) + kb)
                        score_bank(bank[kb], kb, g).then_inc(scores_a, 1)
                    if g >= 1:
                        turn_maxima(g - 1)
                turn_maxima(NG - 1)
                pe.wait_ge(group_max_done, NG * (b + 1))
                pe.nop(nofuse=True)
                pe.transpose(bank[6].bitcast(BF16)[0:KB * NG, 0:P], col_max[:].rearrange("p c g -> p (c g)"),
                             identb[:]).then_inc(col_max_turned, 1)

            def values(b, kb):
                pe.wait_ge(exps, KB * NG * b + NG * (kb + 1))
                for c in range(4):
                    for j in range(4):
                        last = pe.matmul(ps[32 * j:32 * (j + 1), 4 + c, :], v_ones[:, kb, 4 * c + j, :],
                                         probs[:, kb % 2, 4 * c + j, :], start=(kb == 0), stop=(kb == KB - 1),
                                         tile_position=(0, 32 * j), skip_group_check=True)
                last.then_inc(pv_done, 1)

            def attend(b):
                pe.wait_ge(max_in, ONE + 16 * N_MAX * (b + 1))
                pe.wait_ge(v_done, b + 1)
                for kb in range(KB):
                    for g in range(NG):
                        n = kb * NG + g
                        if n >= 4:
                            pe.wait_ge(exps, KB * NG * b + n - 3)
                        score_bank(bank[n % 4], kb, g).then_inc(scores_b, 1)
                        if kb >= 1 and g == 3:
                            values(b, kb - 1)
                values(b, KB - 1)

            def output(b):
                pe.wait_ge(ctx_copied_a, 2 * b + 2)
                pe.wait_ge(ctx_copied_v, 2 * b + 2)
                for n in range(KB):
                    for c in range(4):
                        last = pe.transpose(ps[:, n, P * c:P * (c + 1)], ctx_t[:, c, P * n:P * (n + 1)], ident[:])
                last.then_inc(ctx_turned, 1)
                pe.wait_ge(comb_done, ONE + b + 1)
                turn(lambda n: ps[:, 4, P * n:P * (n + 1)], lambda n: comb[:, n, :], ident[:]).then_inc(comb_turned, 1)
                pe.wait_ge(comb_t_done, b + 1)
                for n in range(KB):
                    last = pe.matmul(ps[:, 5, P * n:P * (n + 1)], comb_t[:, P * n:P * (n + 1)], wo[:],
                                     start=True, stop=True)
                last.then_inc(attn_mm_done, 1)
                pe.wait_ge(h2_done, b + 1)
                turn(lambda n: ps[:, 6, P * n:P * (n + 1)], lambda n: h_nat[:, n, :], ident[:]).then_inc(h2_turned, 1)
                pe.wait_ge(h2_t_done, b + 1)
                for n in range(KB):
                    last = pe.matmul(ps[:, 7, E * n:E * (n + 1)], h2_t[:, P * n:P * (n + 1)], w_router[:],
                                     start=True, stop=True)
                last.then_inc(logits_done, 1)
                pe.wait_ge(combine_done, b + 1)
                turn(lambda n: bank[4].bitcast(BF16)[0:3 * E, P * n:P * (n + 1)],
                     lambda n: combine_pc[:, n, :, :].rearrange("p s e -> p (s e)"), identb[:]).then_inc(combine_turned, 1)

            def experts(b):
                def down(n):
                    if n < BLK:
                        pe.wait_ge(inner_done, BLK * b + n + 1)
                    else:
                        pe.wait_ge(gated_done, ONE + (BLK + 1) * (b + 1))
                    pe.matmul(bank[7], wd[:, n, :], inner[:, n % 2, :], start=(n == 0),
                              stop=(n == BLK)).then_inc(down_mm, 1)

                pe.wait_ge(combine_t_done, b + 1)
                for n in range(BLK + 1):
                    if n >= 2:
                        pe.wait_ge(silu_done, (BLK + 1) * b + n - 1)
                    pe.matmul(bank[3 * (n % 2)], wg[:, n, :], h2_t[:], start=True, stop=True).then_inc(gate_mm, 1)
                    if n >= 2:
                        pe.wait_ge(inner_done, BLK * b + n - 1)
                    last = pe.matmul(bank[3 * (n % 2) + 1], wu[:, n, :], h2_t[:], start=True, stop=True)
                    if n < BLK:
                        last = pe.matmul(bank[3 * (n % 2) + 2],
                                         sel[:, 2 * n:2 * n + 2, :].rearrange("p e i -> p (e i)"), combine_t[:],
                                         start=True, stop=True)
                    last.then_inc(up_mm, 1)
                    if n >= 1:
                        down(n - 1)
                down(BLK)
                pe.wait_ge(y_t_done, b + 1)
                turn(lambda n: ps[:, 6, P * n:P * (n + 1)], lambda n: y_t[:, P * n:P * (n + 1)], ident[:]).then_inc(y_turned, 1)

            with pe.Fori(0, B) as b:
                prepare(b)
                maxima(b)
                attend(b)
                output(b)
                experts(b)


def _layouts(v):
    f = np.float32
    t = lambda w: np.ascontiguousarray(np.asarray(w).T)
    keys_of = np.clip(np.arange(2)[:, None] - (np.arange(TW) - (S - 1))[None, :], -MAX_REL, MAX_REL) + MAX_REL
    table = np.asarray(v["L0_attn_rel_emb"])[keys_of]
    rel = np.zeros((2, SLOT, TW), f)
    for r in range(len(PIECES)):
        rel[:, HD * r:HD * (r + 1)] = table.transpose(0, 2, 1)
    piece_mask = np.zeros((2, SLOT, 3), f)
    for r, (_, pk) in enumerate(PIECES):
        piece_mask[:, HD * r:HD * (r + 1), pk] = 1.0
    mz = np.zeros((P, D + H), f)
    for h in range(H):
        mz[HD * h:HD * (h + 1), HD * h:HD * (h + 1)] = np.asarray(v["L0_attn_M"])[h]
        mz[HD * h:HD * (h + 1), D + h] = np.asarray(v["L0_attn_z"])[h]

    def inner_weights(routed, shared):
        w = np.concatenate([np.asarray(routed).reshape(E * I, D), np.asarray(shared)], 0)
        return np.ascontiguousarray(w.T).reshape(D, BLK + 1, P)

    down = np.asarray(v["L0_ffn_w_down"]).transpose(0, 2, 1).reshape(BLK, P, D)
    down = np.concatenate([down, t(v["L0_ffn_sh_down"])[None]], 0).transpose(1, 0, 2)
    return {
        "x": np.asarray(v["L0_attn_hidden_states"]), "c": np.asarray(v["L0_c"]),
        "ident": np.eye(P, dtype=f), "wq": t(v["L0_attn_Wq"]), "wk": t(v["L0_attn_Wk"]),
        "wv": t(v["L0_attn_Wv"]), "wo": t(v["L0_attn_Wo"]),
        "bq": np.asarray(v["L0_attn_bq"]).reshape(P, 1), "bk": np.asarray(v["L0_attn_bk"]).reshape(P, 1),
        "bv": np.asarray(v["L0_attn_bv"]), "bo": np.asarray(v["L0_attn_bo"]),
        "wmod": np.asarray(v["L0_wmod"]), "mz": mz,
        "gate_alpha": np.asarray(v["L0_attn_gate_alpha"]).reshape(1), "rel": rel.reshape(P, TW),
        "piece_mask": piece_mask.reshape(P, 3), "w_router": t(v["L0_ffn_gate_w"]),
        "b_router": np.asarray(v["L0_ffn_gate_bias"]),
        "wg": inner_weights(v["L0_ffn_w_gate"], v["L0_ffn_sh_gate"]),
        "wu": inner_weights(v["L0_ffn_w_up"], v["L0_ffn_sh_up"]),
        "wd": np.ascontiguousarray(down),
        "sel": np.tile(np.eye(E, dtype=f), (3, 1)),
    }


def kernel(**inputs):
    import concourse.bacc as bacc
    from concourse.bass_utils import run_bass_kernel_spmd

    nc = bacc.Bacc("TRN2", target_bir_lowering=False, num_devices=1)
    arrays, aps = {}, {}
    for name, value in _layouts(inputs).items():
        value = np.ascontiguousarray(value)
        arrays[f"in_{name}"] = value
        aps[name] = nc.dram_tensor(f"in_{name}", value.shape, mybir.dt.from_np(value.dtype),
                                   kind="ExternalInput").ap()
    out = nc.dram_tensor("out", (B, S, D), F32, kind="ExternalOutput").ap()
    build(nc, aps, out)
    result = run_bass_kernel_spmd(nc, [arrays], core_ids=[0])
    return result.results[0]["out"]
```

```python
from contextlib import ExitStack

import numpy as np

import concourse.bass as bass
from concourse import mybir

F32 = mybir.dt.float32
BF16 = mybir.dt.bfloat16
ALU = mybir.AluOpType
ACT = mybir.ActivationFunctionType
AX_X = mybir.AxisListType.X

P = 128
B, S, D = 8, 512, 128
H, HD = 16, 8
HP = H // 2
KB = S // P
QG = 32
NG = S // QG
MAX_REL = 128
SLOT = 64
PIECES = [(0, 0), (0, 1), (0, 2), (1, 0), (1, 1), (2, 0)]
MROW = HD * len(PIECES)
TW = 2 * S
E, I, G = 32, 64, 8
TOPG, TOPK = 4, 8
BLK = E * I // P
BIG = 3.0e38
SCORE_SCALE = float(1.0 / np.sqrt(np.float32(HD)))

NT = 3
UNIT = 8
NU = KB * NG // UNIT
QU = QG * UNIT
ONE = 1
PREP_LINKS, OUT_LINKS = 20, 30


def near(kb, g):
    return abs(kb - g * QG // P) <= 1


def build(nc, a, out):
    ctx = ExitStack()
    with ctx:
        def sb(name, shape, dt=F32):
            return ctx.enter_context(nc.sbuf_tensor(name, shape, dt))

        def sem(name):
            return ctx.enter_context(nc.semaphore(name))

        ident = sb("ident", [P, P])
        identb = sb("identb", [P, P], BF16)
        wq, wk, wv, wo = (sb(n, [P, D]) for n in ("wq", "wk", "wv", "wo"))
        bq, bk = sb("bq", [P, 1]), sb("bk", [P, 1])
        bv, bo = sb("bv", [P, D]), sb("bo", [P, D])
        mz = sb("mz", [P, D + H])
        gate, one_minus_gate = sb("gate", [P, 1]), sb("one_minus_gate", [P, 1])
        gate_in = sb("gate_in", [P, 1])
        minus_half = sb("minus_half", [P, KB])
        rel = sb("rel", [P, TW], BF16)
        rel_lead = sb("rel_lead", [P, TW], BF16)
        rel_far = sb("rel_far", [P, 2])
        own = sb("own", [P, H])
        ownb = sb("ownb", [P, H], BF16)
        piece_mask = sb("piece_mask", [P, 3])
        w_router = sb("w_router", [P, E])
        b_router = sb("b_router", [P, E])
        wg = sb("wg", [P, BLK + 1, P])
        wu = sb("wu", [P, BLK + 1, P])
        wd = sb("wd", [P, BLK + 1, P])
        sel32 = sb("sel32", [3 * E, E])
        sel = sb("sel", [3 * E, E, I], BF16)

        x_pre = sb("x_pre", [P, KB, D])
        mod_pre = sb("mod_pre", [P, 2, D])
        stats = sb("stats", [P, KB, 6])
        mean_var = sb("mean_var", [P, KB, 2])
        rstd = sb("rstd", [P, KB])
        h_norm = sb("h_norm", [P, KB, D])
        h_nat = sb("h_nat", [P, KB, D])
        h_t = sb("h_t", [P, S])
        q_t, k_t, far_t = sb("q_t", [P, S]), sb("k_t", [P, S]), sb("far_t", [P, S])
        rest = sb("rest", [P, S])
        q_pc, k_pc, far_pc = (sb(n, [P, 3, S], BF16) for n in ("q_pc", "k_pc", "far_pc"))
        q_even, q_odd = sb("q_even", [P, 3, S], BF16), sb("q_odd", [P, 3, S], BF16)
        q_lead = sb("q_lead", [P, H, 2 * NG], BF16)
        sigma, sigma_e = sb("sigma", [P, S]), sb("sigma_e", [P, S])
        v_new = sb("v_new", [P, KB, D])
        linear_new = sb("linear_new", [P, KB, D])
        linear_den = sb("linear_den", [P, KB, H])

        lead = sb("lead", [P, H, 2 * NG], BF16)
        content_op = sb("content_op", [P, 2, S], BF16)
        rel_op = sb("rel_op", [P, 2, S], BF16)
        copied = sb("copied", [P, 2, 2, S], BF16)
        half_key_max = sb("half_key_max", [P, 2, 2, S], BF16)
        key_max = sb("key_max", [P, 2, S], BF16)
        col_max = sb("col_max", [P, KB, NG], BF16)
        max_rows = sb("max_rows", [KB * NG, P], BF16)

        v_ones = sb("v_ones", [P, KB, H, 32])
        kst = sb("kst", [P, HP, S], BF16)
        kst_far = sb("kst_far", [P, HP, S], BF16)
        qst = sb("qst", [P, HP, 2, S], BF16)
        qrel = sb("qrel", [P, H, S], BF16)
        probs = sb("probs", [P, 2, H, QU])

        spare = probs[:].rearrange("p a h q -> p (a h q)")
        ctx_t = spare[:, 0:4 * S].rearrange("p (a q) -> p a q", a=4)
        comb = spare[:, 4 * S:5 * S].rearrange("p (n d) -> p n d", d=D)
        comb_t = spare[:, 5 * S:6 * S]
        silu_g = spare[:, 6 * S:8 * S].rearrange("p (a q) -> p a q", a=2)
        gated = spare[:, 8 * S:10 * S].rearrange("p (a q) -> p a q", a=2)
        inner = spare[:, 10 * S:12 * S].rearrange("p (a q) -> p a q", a=2)
        y = spare[:, 12 * S:13 * S].rearrange("p (n d) -> p n d", d=D)
        x_res = sb("x_res", [P, KB, D])
        mod_post = sb("mod_post", [P, 4, D])
        linear = sb("linear", [P, KB, D])
        den_inv = sb("den_inv", [P, KB * H])
        attn = sb("attn", [P, KB, D])
        x1 = sb("x1", [P, KB, D])
        h2_nat = sb("h2_nat", [P, KB, D])
        h2_t = sb("h2_t", [P, S])
        score = sb("score", [P, KB, E])
        biased = sb("biased", [P, KB, E])
        pair_hi, pair_lo = sb("pair_hi", [P, KB * G, 2]), sb("pair_lo", [P, KB * G, 2])
        top1, top2 = sb("top1", [P, KB * G]), sb("top2", [P, KB * G])
        low_hi, hi_lo = sb("low_hi", [P, KB * G]), sb("hi_lo", [P, KB * G])
        group_sum = sb("group_sum", [P, KB, G + 4])
        group_top = sb("group_top", [P, KB, 8])
        group_left = sb("group_left", [P, KB, G + 4])
        group_mask = sb("group_mask", [P, KB, G])
        masked = sb("masked", [P, KB, E])
        expert_top = sb("expert_top", [P, KB, 8])
        expert_left = sb("expert_left", [P, KB, E])
        chosen = sb("chosen", [P, KB, E])
        weight = sb("weight", [P, KB, E])
        weight_sum = sb("weight_sum", [P, KB])
        combine = sb("combine", [P, KB, E])
        combine_rest = sb("combine_rest", [P, KB, E])
        combine_pc = sb("combine_pc", [P, KB, 3, E], BF16)
        combine_t = sb("combine_t", [3 * E, S], BF16)
        y_t = sb("y_t", [P, S])

        rel32 = spare[:, 0:TW]
        rel_rest = spare[:, TW:2 * TW]
        rel_lead32 = spare[:, 2 * TW:3 * TW]
        wmod = spare[:, 3 * TW:3 * TW + 6 * D]
        c_t = spare[:, 4 * TW:4 * TW + B]
        silu_c = spare[:, 4 * TW + B:4 * TW + 2 * B]
        mod = spare[0:B, 5 * TW:5 * TW + 6 * D].rearrange("b (m d) -> b m d", d=D)
        mod_mag = spare[0:B, 6 * TW:6 * TW + 2 * D].rearrange("b (m d) -> b m d", d=D)
        rel_piece = spare[:, 7 * TW:7 * TW + TW // 2].bitcast(BF16)

        ps = ctx.enter_context(nc.psum_tensor("ps", [P, 8, 512], F32))
        bank = [ps[:, n, :] for n in range(8)]

        k_dram = nc.dram_tensor("k_pieces", [2, 3, D, S], BF16, kind="Internal").ap()
        q_dram = nc.dram_tensor("q_pieces", [3, 3, D, S], BF16, kind="Internal").ap()
        lead_dram = nc.dram_tensor("q_lead_rows", [H, D, 2 * NG], BF16, kind="Internal").ap()
        mod_dram = nc.dram_tensor("mod_rows", [B, 6, D], F32, kind="Internal").ap()

        weights_in, pool_set, vec_set = sem("weights_in"), sem("pool_set"), sem("vec_set")
        consts_chain, consts_ready = sem("consts_chain"), sem("consts_ready")
        silu_c_done, gate_act, mod_mm, mod_rows_done, mod_stored = (
            sem(n) for n in ("silu_c_done", "gate_act", "mod_mm", "mod_rows_done", "mod_stored"))
        x_in, var_done, rstd_done, h_done, h_turned, h_t_done = (
            sem(n) for n in ("x_in", "var_done", "rstd_done", "h_done", "h_turned", "h_t_done"))
        q_mm, k_mm, v_mm, q_biased, k_biased, v_new_done = (
            sem(n) for n in ("q_mm", "k_mm", "v_mm", "q_biased", "k_biased", "v_new_done"))
        q_pieces_done, k_pieces_done, far_pieces_done, q_copies_done = (
            sem(n) for n in ("q_pieces_done", "k_pieces_done", "far_pieces_done", "q_copies_done"))
        pieces_stored, lead_in, stacks_in = sem("pieces_stored"), sem("lead_in"), sem("stacks_in")
        neg_part_done, neg_exp_done, sigma_done, linear_mm, linear_halves = (
            sem(n) for n in ("neg_part_done", "neg_exp_done", "sigma_done", "linear_mm", "linear_halves"))
        prep_chain, out_chain = sem("prep_chain"), sem("out_chain")
        operands_a, scores_a, scores_copied, half_maxima, key_maxima = (
            sem(n) for n in ("operands_a", "scores_a", "scores_copied", "half_maxima", "key_maxima"))
        max_turned, group_maxima, col_max_turned, max_rows_done, max_in = (
            sem(n) for n in ("max_turned", "group_maxima", "col_max_turned", "max_rows_done", "max_in"))
        handed_over, scores_b, exps, pv_done = (sem(n) for n in ("handed_over", "scores_b", "exps", "pv_done"))
        res_in, ctx_copied_a, ctx_copied_v, ctx_turned = (
            sem(n) for n in ("res_in", "ctx_copied_a", "ctx_copied_v", "ctx_turned"))
        comb_done, comb_turned, comb_t_done, attn_mm, residual_done = (
            sem(n) for n in ("comb_done", "comb_turned", "comb_t_done", "attn_mm", "residual_done"))
        var2_done, rstd2_done, h2_done, h2_turned, h2_t_done = (
            sem(n) for n in ("var2_done", "rstd2_done", "h2_done", "h2_turned", "h2_t_done"))
        logits_done, sigmoid_done, combine_done, combine_turned, combine_t_done = (
            sem(n) for n in ("logits_done", "sigmoid_done", "combine_done", "combine_turned", "combine_t_done"))
        gate_mm, up_mm, spread_mm, silu_done, gated_done, inner_done, down_mm = (
            sem(n) for n in ("gate_mm", "up_mm", "spread_mm", "silu_done", "gated_done", "inner_done", "down_mm"))
        y_t_done, y_turned, y_done, x2_done, stored = (
            sem(n) for n in ("y_t_done", "y_turned", "y_done", "x2_done", "stored"))
        carried = [h_done, x2_done, q_copies_done, stacks_in, operands_a, scores_b, pieces_stored, scores_a,
                   half_maxima, col_max_turned, max_in, exps, pv_done, comb_done, sigma_done,
                   h_turned, far_pieces_done, down_mm, gated_done, stored, linear_halves, linear_mm, handed_over]

        weight_loads = [
            (rel32, a["rel"]), (rel_lead32, a["rel_lead"]), (piece_mask[:], a["piece_mask"]),
            (c_t, a["c"]), (wmod, a["wmod"]),
            (ident[:], a["ident"]), (wq[:], a["wq"]), (wk[:], a["wk"]), (wv[:], a["wv"]), (wo[:], a["wo"]),
            (bq[:], a["bq"]), (bk[:], a["bk"]), (bv[:], a["bv"].partition_broadcast(P)),
            (bo[:], a["bo"].partition_broadcast(P)), (mz[:], a["mz"]),
            (gate_in[:], a["gate_alpha"].partition_broadcast(P)), (rel_far[:], a["rel_far"]),
            (own[:], a["own"]), (w_router[:], a["w_router"]),
            (b_router[:], a["b_router"].partition_broadcast(P)), (sel32[:], a["sel"]),
            (wg[:], a["wg"]), (wu[:], a["wu"]), (wd[:], a["wd"]),
        ]
        ALL_WEIGHTS = 16 * len(weight_loads)
        N_STORES = 6
        RUNS = [(0, 3, 0, 0), (3, 2, 1, 0), (5, 1, 2, 0)]
        N_STACK = 2 * (len(PIECES) + 3 * len(RUNS))
        N_MAX = 4 * 4

        TURN_H, MM_Q, MM_K, MM_V, EXP_NEG, MM_LIN0, MM_LIN1 = 14, 20, 26, 32, 36, 42, 48
        CTX, COMB, ATTN, NORM, TURN_H2, ROUTE, WEIGHTS = 0, 1, 3, 4, 5, 6, 10
        SLOTS = WEIGHTS + BLK + 1

        block = ctx.enter_context(nc.Block())

        @block.sync
        def _(sp):
            for dst, src in weight_loads:
                sp.dma_start(dst, src).then_inc(weights_in, 16)
            sp.wait_ge(mod_rows_done, 1)
            sp.dma_start(mod_dram, mod).then_inc(mod_stored, 16)
            sp.wait_ge(mod_stored, 16)
            sp.wait_ge(pool_set, 6)

            def load_for_prepare(b):
                sp.wait_ge(h_done, ONE + b)
                sp.nop(nofuse=True)
                sp.dma_start(x_pre[:], a["x"][bass.ds(b, 1)].rearrange("o (n p) d -> p (o n) d", p=P)).then_inc(x_in, 16)
                sp.dma_start(mod_pre[:], mod_dram[bass.ds(b, 1), 0:2].broadcast_to([P, 2, D])).then_inc(x_in, 16)

            def load_for_output(b):
                sp.wait_ge(x2_done, ONE + b)
                sp.nop(nofuse=True)
                sp.dma_start(x_res[:], a["x"][bass.ds(b, 1)].rearrange("o (n p) d -> p (o n) d", p=P)).then_inc(res_in, 16)
                sp.dma_start(mod_post[:], mod_dram[bass.ds(b, 1), 2:6].broadcast_to([P, 4, D])).then_inc(res_in, 16)

            def store_pieces(b):
                sp.wait_ge(stacks_in, ONE + 16 * N_STACK * b)
                sp.nop(nofuse=True)
                sp.wait_ge(q_pieces_done, b + 1)
                sp.dma_start(q_dram[0].rearrange("r p q -> p r q"), q_pc[:]).then_inc(pieces_stored, 16)
                sp.wait_ge(k_pieces_done, b + 1)
                sp.dma_start(k_dram[0].rearrange("r p q -> p r q"), k_pc[:]).then_inc(pieces_stored, 16)
                sp.wait_ge(q_copies_done, ONE + 3 * b + 3)
                sp.dma_start(lead_dram.rearrange("i p j -> p i j"), q_lead[:]).then_inc(pieces_stored, 16)
                sp.dma_start(q_dram[1].rearrange("r p q -> p r q"), q_even[:]).then_inc(pieces_stored, 16)
                sp.dma_start(q_dram[2].rearrange("r p q -> p r q"), q_odd[:]).then_inc(pieces_stored, 16)
                sp.wait_ge(far_pieces_done, ONE + b + 1)
                sp.dma_start(k_dram[1].rearrange("r p q -> p r q"), far_pc[:]).then_inc(pieces_stored, 16)
                sp.wait_ge(pieces_stored, ONE + 16 * N_STORES * (b + 1))
                sp.nop(nofuse=True)
                sp.wait_ge(operands_a, ONE + 2 * NG * b)
                sp.dma_start(lead[:].rearrange("p h j -> p (h j)"), lead_dram.rearrange("i (d h) j -> d i (h j)", d=HD)).then_inc(lead_in, 16)

            def load_stacks(b):
                sp.wait_ge(scores_b, ONE + KB * NG * b)
                for s in range(2):
                    for r, (pq, _) in enumerate(PIECES):
                        rows = slice(SLOT * s + HD * r, SLOT * s + HD * (r + 1))
                        sp.dma_start(qst[rows, :, s, :], q_dram[0, pq].rearrange("(d a s) q -> s d a q", d=HD, s=2)[s]
                                     ).then_inc(stacks_in, 16)
                    for r, n, pq, pk in RUNS:
                        rows = slice(SLOT * s + HD * r, SLOT * s + HD * (r + n))
                        for dst, keys in ((kst, k_dram[0]), (kst_far, k_dram[1])):
                            sp.dma_start(dst[rows], keys[pk:pk + n].rearrange("r (d a s) q -> s (r d) a q", d=HD, s=2)[s]
                                         ).then_inc(stacks_in, 16)
                        sp.dma_start(qrel[rows].rearrange("p h q -> p (h q)"),
                                     q_dram[1 + s, pq].rearrange("(d h) q -> d (h q)", d=HD).unsqueeze(0).broadcast_to(
                                         [n, HD, H * S])).then_inc(stacks_in, 16)

            def load_maxima(b):
                sp.wait_ge(max_rows_done, b + 1)
                for c in range(4):
                    for s in range(2):
                        for p2 in range(2):
                            sp.dma_start(
                                qst[SLOT * s + MROW:SLOT * s + MROW + 1, 2 * c + p2, s, :],
                                max_rows[NG * c:NG * (c + 1), (2 * p2 + s) * QG:(2 * p2 + s + 1) * QG],
                            ).then_inc(max_in, 16)

            def store_out(b):
                sp.wait_ge(x2_done, ONE + b + 1)
                sp.nop(nofuse=True)
                sp.dma_start(out[bass.ds(b, 1)].rearrange("o (n p) d -> p (o n) d", p=P), x1[:]).then_inc(stored, 16)

            load_for_prepare(0)
            store_pieces(0)
            load_stacks(0)
            load_maxima(0)
            with sp.Fori(0, B - 1) as t:
                load_for_output(t)
                load_for_prepare(t + 1)
                store_pieces(t + 1)
                load_stacks(t + 1)
                load_maxima(t + 1)
                store_out(t)
            load_for_output(B - 1)
            store_out(B - 1)
            sp.wait_ge(stored, ONE + 16 * B)

        @block.gpsimd
        def _(pool):
            for s in carried:
                pool.sem_inc(s, ONE)
            pool.memset(minus_half[:], -0.5).then_inc(pool_set, 1)
            pool.memset(q_even[:], 0.0).then_inc(pool_set, 1)
            pool.memset(q_odd[:], 0.0).then_inc(pool_set, 1)
            pool.memset(kst[:], 1.0).then_inc(pool_set, 1)
            pool.memset(kst_far[:], 1.0).then_inc(pool_set, 1)
            pool.memset(qst[:], 0.0).then_inc(pool_set, 1)
            pool.memset(qrel[:], 0.0).then_inc(pool_set, 1)
            pool.wait_ge(pool_set, 7)
            pool.wait_ge(consts_ready, 1)

            def prepare(b):
                pool.wait_ge(var_done, b + 1)
                pool.tensor_tensor(rstd[:], mean_var[:, :, 1], minus_half[:], ALU.pow).then_inc(rstd_done, 1)
                pool.wait_ge(q_pieces_done, b + 1)
                pool.nop(nofuse=True)
                pool.wait_ge(pieces_stored, ONE + 16 * N_STORES * b)
                pool.nop(nofuse=True)
                pool.tensor_copy(q_lead[:], q_pc[:, 0, :].rearrange("p (j i) -> p i j", i=H)).then_inc(q_copies_done, 1)
                for parity, dst in enumerate((q_even, q_odd)):
                    pool.tensor_copy(dst[:, :, parity:S:2], q_pc[:, :, parity:S:2]).then_inc(q_copies_done, 1)

            def group_operands(b, g):
                if g == 0:
                    pool.wait_ge(lead_in, 16 * (b + 1))
                    pool.nop(nofuse=True)
                pool.wait_ge(scores_a, ONE + KB * NG * b + KB * max(g - 1, 0))
                pool.tensor_tensor(content_op[:, g % 2, :].rearrange("p (h q) -> p h q", q=QG),
                                   q_pc[:, 0, QG * g:QG * (g + 1)].unsqueeze(1).broadcast_to([P, H, QG]),
                                   ownb[:].unsqueeze(2).broadcast_to([P, H, QG]), ALU.mult).then_inc(operands_a, 1)
                for u in range(2):
                    last = pool.tensor_tensor(rel_op[:, g % 2, 256 * u:256 * (u + 1)].rearrange("p (h i) -> p h i", i=H),
                                              lead[:, :, 2 * g + u:2 * g + u + 1].broadcast_to([P, H, H]),
                                              ownb[:].unsqueeze(1).broadcast_to([P, H, H]), ALU.mult)
                last.then_inc(operands_a, 1)

            def second_norm(b):
                pool.wait_ge(var2_done, b + 1)
                pool.tensor_tensor(rstd[:], mean_var[:, :, 1], minus_half[:], ALU.pow).then_inc(rstd2_done, 1)

            prepare(0)
            for g in range(NG):
                group_operands(0, g)
            with pool.Fori(0, B - 1) as t:
                prepare(t + 1)
                for g in range(NG):
                    group_operands(t + 1, g)
                    if g == ATTN + 1:
                        second_norm(t)
            second_norm(B - 1)

        @block.scalar
        def _(act):
            act.wait_ge(weights_in, ALL_WEIGHTS)
            act.activation(silu_c, c_t, ACT.Silu).then_inc(silu_c_done, 1)
            act.activation(gate[:], gate_in[:], ACT.Sigmoid).then_inc(gate_act, 1)

            def turned_h(b):
                act.wait_ge(h_turned, ONE + b + 1)
                act.copy(h_t[:], bank[3]).then_inc(h_t_done, 1)

            def bias_q(b):
                act.wait_ge(sigma_done, ONE + b)
                act.wait_ge(q_mm, b + 1)
                act.activation(q_t[:], bank[3], ACT.Identity, bias=bq[:]).then_inc(q_biased, 1)

            def bias_k(b):
                act.wait_ge(far_pieces_done, ONE + b)
                act.wait_ge(k_mm, b + 1)
                act.activation(k_t[:], bank[3], ACT.Identity, bias=bk[:]).then_inc(k_biased, 1)

            def exp_negative(b):
                act.wait_ge(neg_part_done, b + 1)
                act.activation(sigma_e[:], sigma[:], ACT.Exp).then_inc(neg_exp_done, 1)

            def copy_scores(b, g):
                for kb in (0, 2):
                    act.wait_ge(half_maxima, ONE + 2 * NG * b + (2 * (g - 2) + kb // 2 + 1 if g >= 2 else 0))
                    act.wait_ge(scores_a, ONE + KB * NG * b + KB * g + kb + 1)
                    act.copy(copied[:, g % 2, kb // 2, :], bank[(KB * g + kb) % NT]).then_inc(scores_copied, 1)

            def attend(b, prepare_next):
                for n in range(KB * NG):
                    kb, g, u = n // NG, n % NG, n // UNIT
                    if n % UNIT == 0:
                        act.wait_ge(pv_done, ONE + NU * b + max(u - 1, 0))
                    if n == UNIT:
                        act.wait_ge(x2_done, ONE + b)
                    act.wait_ge(scores_b, ONE + KB * NG * b + n + 1)
                    q0 = QG * (g % UNIT)
                    act.activation(probs[:, u % 2, :, q0:q0 + QG], bank[n % NT].rearrange("p (h q) -> p h q", q=QG),
                                   ACT.Exp, scale=SCORE_SCALE).then_inc(exps, 1)
                    if prepare_next and n == TURN_H:
                        turned_h(b + 1)
                    if prepare_next and n == MM_Q:
                        bias_q(b + 1)
                    if prepare_next and n == MM_K:
                        bias_k(b + 1)
                    if prepare_next and n == EXP_NEG:
                        exp_negative(b + 1)

            def after_attend(b, maxima_next):
                act.wait_ge(pv_done, ONE + NU * (b + 1))
                for c in range(2):
                    act.copy(ctx_t[:, c, :], bank[4 + c]).then_inc(ctx_copied_a, 1)
                for k in range(SLOTS):
                    if maxima_next and k < NG:
                        copy_scores(b + 1, k)
                    if k == COMB + 1:
                        act.wait_ge(comb_turned, b + 1)
                        act.copy(comb_t, bank[4]).then_inc(comb_t_done, 1)
                    if k == TURN_H2:
                        act.wait_ge(h2_turned, b + 1)
                        act.copy(h2_t[:], bank[6]).then_inc(h2_t_done, 1)
                    if k == ROUTE:
                        act.wait_ge(logits_done, b + 1)
                        act.activation(score[:], ps[:, 7, 0:KB * E].rearrange("p (n e) -> p n e", e=E),
                                       ACT.Sigmoid).then_inc(sigmoid_done, 1)
                    if k == WEIGHTS:
                        act.wait_ge(combine_turned, b + 1)
                        act.copy(combine_t[:], bank[6].bitcast(BF16)[0:3 * E, 0:S]).then_inc(combine_t_done, 1)
                    if k >= WEIGHTS:
                        n = k - WEIGHTS
                        act.wait_ge(gate_mm, (BLK + 1) * b + n + 1)
                        act.wait_ge(gated_done, ONE + (BLK + 1) * b + max(n - 1, 0))
                        act.activation(silu_g[:, n % 2, :], bank[4], ACT.Silu).then_inc(silu_done, 1)
                act.wait_ge(down_mm, ONE + (BLK + 1) * (b + 1))
                act.copy(y_t[:], bank[7]).then_inc(y_t_done, 1)

            turned_h(0)
            bias_q(0)
            bias_k(0)
            exp_negative(0)
            for g in range(NG):
                copy_scores(0, g)
            with act.Fori(0, B - 1) as t:
                attend(t, True)
                after_attend(t, True)
            attend(B - 1, False)
            after_attend(B - 1, False)

        @block.vector
        def _(dve):
            dve.memset(v_ones[:], 0.0).then_inc(vec_set, 1)
            dve.wait_ge(vec_set, 1)
            dve.memset(v_ones[:, :, :, HD:HD + 1], 1.0).then_inc(vec_set, 1)
            dve.memset(group_sum[:, :, G:G + 4], BIG).then_inc(vec_set, 1)
            dve.wait_ge(weights_in, ALL_WEIGHTS)
            dve.tensor_copy(ownb[:], own[:]).then_inc(consts_ready, 1)
            dve.tensor_copy(identb[:], ident[:]).then_inc(consts_ready, 1)
            dve.tensor_copy(rel_lead[:], rel_lead32).then_inc(consts_ready, 1)
            dve.tensor_copy(sel[:], sel32[:].unsqueeze(2).broadcast_to([3 * E, E, I])).then_inc(consts_ready, 1)
            consts = 0

            def const_link(ins):
                nonlocal consts
                consts += 1
                ins.then_inc(consts_chain, 1)
                dve.wait_ge(consts_chain, consts)

            dve.wait_ge(mod_mm, 1)
            dve.tensor_copy(mod[:, 0:3, :], ps[0:B, 0, 0:3 * D].rearrange("p (m d) -> p m d", d=D))
            const_link(dve.tensor_copy(mod[:, 3:6, :], ps[0:B, 1, 0:3 * D].rearrange("p (m d) -> p m d", d=D)))
            const_link(dve.tensor_scalar(mod[:, 1:5:3, :], mod[:, 1:5:3, :], 1.0, None, ALU.add))
            const_link(dve.tensor_scalar(mod_mag, mod[:, 2:6:3, :], -1.0, 0.25, ALU.mult, ALU.max))
            const_link(dve.tensor_tensor(mod_mag, mod_mag, mod[:, 2:6:3, :], ALU.max))
            const_link(dve.tensor_scalar(mod[:, 2:6:3, :], mod[:, 2:6:3, :], 0.0, 2.0, ALU.is_ge, ALU.mult))
            dve.scalar_tensor_tensor(mod[:, 2:6:3, :], mod[:, 2:6:3, :], 1.0, mod_mag,
                                     ALU.subtract, ALU.mult).then_inc(mod_rows_done, 1)
            const_link(dve.tensor_copy(rel_piece, rel32))
            const_link(dve.tensor_scalar(rel[:], rel_piece, piece_mask[:, 0:1], None, ALU.mult))
            for piece in (1, 2):
                left = rel32 if piece == 1 else rel_rest
                const_link(dve.tensor_tensor(rel_rest, left, rel_piece, ALU.subtract))
                const_link(dve.tensor_copy(rel_piece, rel_rest))
                const_link(dve.scalar_tensor_tensor(rel[:], rel_piece, piece_mask[:, piece:piece + 1], rel[:],
                                                    ALU.mult, ALU.add))
            dve.wait_ge(gate_act, 1)
            dve.tensor_scalar(one_minus_gate[:], gate[:], -1.0, 1.0, ALU.mult, ALU.add).then_inc(consts_ready, 1)
            dve.wait_ge(consts_ready, 5)

            def row(tile, m):
                return tile[:, m, :].unsqueeze(1).broadcast_to([P, KB, D])

            def variance(link, src, ready):
                for n in range(KB):
                    last = dve.bn_stats(stats[:, n, :], src[:, n, :])
                link(last)
                dve.nop(nofuse=True)
                for n in range(KB):
                    last = dve.bn_aggr(mean_var[:, n, :], stats[:, n, :])
                link(last)
                dve.tensor_scalar(mean_var[:, :, 1], mean_var[:, :, 1], 1e-5, None, ALU.add).then_inc(ready, 1)

            def normalise(link, src, dst, to, shift, scale, done):
                for n in range(KB):
                    last = dve.tensor_scalar(dst[:, n, :], src[:, n, :], mean_var[:, n, 0:1], rstd[:, n:n + 1],
                                             ALU.subtract, ALU.mult)
                link(last)
                link(dve.tensor_tensor(to[:], dst[:], scale, ALU.mult))
                dve.tensor_tensor(to[:], to[:], shift, ALU.add).then_inc(done, 1)

            def prepare(b):
                count = 0

                def link(ins):
                    nonlocal count
                    count += 1
                    ins.then_inc(prep_chain, 1)
                    dve.wait_ge(prep_chain, PREP_LINKS * b + count)

                dve.wait_ge(x_in, 32 * (b + 1))
                variance(link, x_pre, var_done)
                dve.wait_ge(rstd_done, b + 1)
                dve.wait_ge(h_turned, ONE + b)
                normalise(link, x_pre, h_norm, h_nat, row(mod_pre, 0), row(mod_pre, 1), h_done)

                def split(src, pc, done):
                    link(dve.tensor_copy(pc[:, 0, :], src[:]))
                    link(dve.tensor_tensor(rest[:], src[:], pc[:, 0, :], ALU.subtract))
                    link(dve.tensor_copy(pc[:, 1, :], rest[:]))
                    dve.tensor_tensor(pc[:, 2, :], rest[:], pc[:, 1, :], ALU.subtract).then_inc(done, 1)

                dve.wait_ge(pieces_stored, ONE + 16 * N_STORES * b)
                dve.wait_ge(q_copies_done, ONE + 3 * b)
                dve.wait_ge(operands_a, ONE + 2 * NG * b)
                dve.wait_ge(q_biased, b + 1)
                split(q_t, q_pc, q_pieces_done)
                dve.wait_ge(linear_mm, ONE + 2 * b)
                dve.tensor_scalar(sigma[:], q_t[:], 0.0, None, ALU.min).then_inc(neg_part_done, 1)
                dve.wait_ge(q_pieces_done, b + 1)
                dve.wait_ge(scores_a, ONE + KB * NG * b)
                dve.wait_ge(k_biased, b + 1)
                split(k_t, k_pc, k_pieces_done)
                for far in range(2):
                    half = slice(far * S // 2, (far + 1) * S // 2)
                    last = dve.tensor_scalar(far_t[:, half], k_t[:, half], rel_far[:, far:far + 1], None, ALU.add)
                link(last)
                dve.wait_ge(k_pieces_done, b + 1)
                split(far_t, far_pc, far_pieces_done)
                dve.wait_ge(handed_over, ONE + 2 * b)
                dve.wait_ge(v_mm, b + 1)
                dve.tensor_tensor(v_new[:], bank[3].rearrange("p (n d) -> p n d", d=D),
                                  bv[:].unsqueeze(1).broadcast_to([P, KB, D]), ALU.add).then_inc(v_new_done, 1)
                dve.wait_ge(neg_exp_done, b + 1)
                dve.scalar_tensor_tensor(sigma[:], q_t[:], 0.0, sigma_e[:], ALU.max, ALU.add).then_inc(sigma_done, 1)
                for half in range(2):
                    dve.wait_ge(linear_mm, ONE + 2 * b + half + 1)
                    two = ps[:, 3, 0:2 * (D + H)].rearrange("p (n m) -> p n m", m=D + H)
                    den = linear_den[:, 2 * half:2 * half + 2, :]
                    link(dve.tensor_scalar(den, two[:, :, D:D + H], 1e-6, None, ALU.add))
                    link(dve.reciprocal(den, den))
                    link(dve.tensor_scalar(den, den, one_minus_gate[:], None, ALU.mult))
                    dve.tensor_tensor(
                        linear_new[:, 2 * half:2 * half + 2, :].rearrange("p n (h d) -> p n h d", d=HD),
                        two[:, :, 0:D].rearrange("p n (h d) -> p n h d", d=HD),
                        den.unsqueeze(3).broadcast_to([P, 2, H, HD]), ALU.mult).then_inc(linear_halves, 1)
                if count != PREP_LINKS:
                    raise ValueError(f"PREP_LINKS is {count}")

            def hand_over(b):
                dve.wait_ge(v_new_done, b + 1)
                dve.wait_ge(pv_done, ONE + NU * b)
                dve.tensor_copy(v_ones[:, :, :, 0:HD].rearrange("p n h d -> p (n h) d"),
                                v_new[:].rearrange("p n (h d) -> p (n h) d", d=HD)).then_inc(handed_over, 1)
                dve.wait_ge(linear_halves, ONE + 2 * (b + 1))
                dve.wait_ge(comb_done, ONE + b)
                dve.tensor_copy(linear[:], linear_new[:]).then_inc(handed_over, 1)

            def group_halves(b, g):
                for half in range(2):
                    n = KB * g + 2 * half + 1
                    dve.wait_ge(scores_copied, 2 * NG * b + 2 * g + half + 1)
                    dve.wait_ge(scores_a, ONE + KB * NG * b + n + 1)
                    dve.tensor_tensor(half_key_max[:, g % 2, half, :], bank[n % NT], copied[:, g % 2, half, :],
                                      ALU.max).then_inc(half_maxima, 1)
                if g >= 2:
                    dve.wait_ge(max_turned, NG * b + g - 1)
                dve.wait_ge(half_maxima, ONE + 2 * NG * b + 2 * g + 2)
                dve.tensor_tensor(key_max[:, g % 2, :], half_key_max[:, g % 2, 0, :], half_key_max[:, g % 2, 1, :],
                                  ALU.max).then_inc(key_maxima, 1)

            def group_reduce(b, g):
                if g == 0:
                    dve.wait_ge(col_max_turned, ONE + b)
                dve.wait_ge(max_turned, NG * b + g + 1)
                dve.tensor_reduce(col_max[:, :, g], bank[3].bitcast(BF16)[:, 0:KB * P].rearrange(
                    "p (c k) -> p c k", k=P), AX_X, ALU.max).then_inc(group_maxima, 1)

            def negate_maxima(b):
                dve.wait_ge(max_in, ONE + 16 * N_MAX * b)
                dve.wait_ge(col_max_turned, ONE + b + 1)
                dve.tensor_scalar(max_rows[:], bank[3].bitcast(BF16)[0:KB * NG, 0:P], -1.0, None,
                                  ALU.mult).then_inc(max_rows_done, 1)

            def after_attend(b, maxima_next):
                count = 0

                def link(ins):
                    nonlocal count
                    count += 1
                    ins.then_inc(out_chain, 1)
                    dve.wait_ge(out_chain, OUT_LINKS * b + count)

                def combine_heads():
                    dve.wait_ge(ctx_turned, b + 1)
                    local = ps[:, 4:8, :].rearrange("p n (h m) -> p (n h) m", m=32)
                    link(dve.reciprocal(den_inv[:], local[:, :, HD]))
                    link(dve.tensor_scalar(den_inv[:], den_inv[:], gate[:], None, ALU.mult))
                    link(dve.tensor_tensor(comb.rearrange("p n (h d) -> p (n h) d", d=HD), local[:, :, 0:HD],
                                           den_inv[:].unsqueeze(2).broadcast_to([P, KB * H, HD]), ALU.mult))
                    dve.tensor_tensor(comb, comb, linear[:], ALU.add).then_inc(comb_done, 1)

                def residual():
                    dve.wait_ge(res_in, 32 * (b + 1))
                    dve.wait_ge(attn_mm, b + 1)
                    link(dve.tensor_tensor(attn[:], bank[5].rearrange("p (n d) -> p n d", d=D),
                                           bo[:].unsqueeze(1).broadcast_to([P, KB, D]), ALU.add))
                    link(dve.tensor_tensor(attn[:], attn[:], row(mod_post, 0), ALU.mult))
                    dve.wait_ge(stored, ONE + 16 * b)
                    dve.tensor_tensor(x1[:], attn[:], x_res[:], ALU.add).then_inc(residual_done, 1)
                    dve.wait_ge(residual_done, b + 1)

                def rank_groups():
                    dve.wait_ge(sigmoid_done, b + 1)
                    link(dve.tensor_tensor(biased[:], score[:], b_router[:].unsqueeze(1).broadcast_to([P, KB, E]),
                                           ALU.add))
                    quads = biased[:].rearrange("p n (g j two) -> p (n g) j two", j=2, two=2)
                    dve.tensor_tensor(pair_hi[:], quads[:, :, :, 0], quads[:, :, :, 1], ALU.max)
                    link(dve.tensor_tensor(pair_lo[:], quads[:, :, :, 0], quads[:, :, :, 1], ALU.min))
                    dve.tensor_tensor(top1[:], pair_hi[:, :, 0], pair_hi[:, :, 1], ALU.max)
                    dve.tensor_tensor(low_hi[:], pair_hi[:, :, 0], pair_hi[:, :, 1], ALU.min)
                    link(dve.tensor_tensor(hi_lo[:], pair_lo[:, :, 0], pair_lo[:, :, 1], ALU.max))
                    link(dve.tensor_tensor(top2[:], low_hi[:], hi_lo[:], ALU.max))
                    link(dve.tensor_tensor(group_sum[:, :, 0:G], top1[:].rearrange("p (n g) -> p n g", g=G),
                                           top2[:].rearrange("p (n g) -> p n g", g=G), ALU.add))
                    dve.nop(nofuse=True)
                    for n in range(KB):
                        last = dve.max(group_top[:, n, :], group_sum[:, n, :])
                    link(last)
                    dve.nop(nofuse=True)
                    for n in range(KB):
                        last = dve.match_replace(group_left[:, n, :], group_top[:, n, :], group_sum[:, n, :], -BIG)
                    link(last)

                def choose_experts():
                    link(dve.tensor_scalar(group_mask[:], group_left[:, :, 0:G], -0.5 * BIG, None, ALU.is_le))
                    link(dve.tensor_tensor(masked[:].rearrange("p n (g j) -> p (n g) j", g=G),
                                           biased[:].rearrange("p n (g j) -> p (n g) j", g=G),
                                           group_mask[:].rearrange("p n g -> p (n g)").unsqueeze(2).broadcast_to(
                                               [P, KB * G, E // G]), ALU.mult))
                    dve.nop(nofuse=True)
                    for n in range(KB):
                        last = dve.max(expert_top[:, n, :], masked[:, n, :])
                    link(last)
                    dve.nop(nofuse=True)
                    for n in range(KB):
                        last = dve.match_replace(expert_left[:, n, :], expert_top[:, n, :], masked[:, n, :], -BIG)
                    link(last)
                    link(dve.tensor_scalar(chosen[:], expert_left[:], -0.5 * BIG, None, ALU.is_le))

                def weigh_experts():
                    link(dve.tensor_tensor(weight[:], score[:], chosen[:], ALU.mult))
                    link(dve.tensor_reduce(weight_sum[:], weight[:], AX_X, ALU.add))
                    link(dve.tensor_scalar(weight_sum[:], weight_sum[:], 1e-20, None, ALU.add))
                    link(dve.reciprocal(weight_sum[:], weight_sum[:]))
                    link(dve.tensor_tensor(combine[:], weight[:], weight_sum[:].unsqueeze(2).broadcast_to([P, KB, E]),
                                           ALU.mult))
                    link(dve.tensor_scalar(combine[:], combine[:], 2.5, None, ALU.mult))
                    link(dve.tensor_copy(combine_pc[:, :, 0, :], combine[:]))
                    link(dve.tensor_tensor(combine_rest[:], combine[:], combine_pc[:, :, 0, :], ALU.subtract))
                    link(dve.tensor_copy(combine_pc[:, :, 1, :], combine_rest[:]))
                    dve.tensor_tensor(combine_pc[:, :, 2, :], combine_rest[:], combine_pc[:, :, 1, :],
                                      ALU.subtract).then_inc(combine_done, 1)

                def expert_block(n):
                    e = (BLK + 1) * b + n
                    dve.wait_ge(down_mm, ONE + (BLK + 1) * b + max(n - 1, 0))
                    dve.wait_ge(silu_done, e + 1)
                    dve.wait_ge(up_mm, e + 1)
                    dst = gated if n < BLK else inner
                    dve.tensor_tensor(dst[:, n % 2, :], bank[5], silu_g[:, n % 2, :], ALU.mult).then_inc(gated_done, 1)
                    if n < BLK:
                        dve.wait_ge(spread_mm, BLK * b + n + 1)
                        dve.wait_ge(gated_done, ONE + e + 1)
                        dve.tensor_tensor(inner[:, n % 2, :], bank[6], gated[:, n % 2, :],
                                          ALU.mult).then_inc(inner_done, 1)

                dve.wait_ge(pv_done, ONE + NU * (b + 1))
                for c in range(2, 4):
                    dve.tensor_copy(ctx_t[:, c, :], bank[4 + c]).then_inc(ctx_copied_v, 1)
                for k in range(SLOTS):
                    if maxima_next and k < NG:
                        group_halves(b + 1, k)
                    if maxima_next and 1 <= k <= NG:
                        group_reduce(b + 1, k - 1)
                    if maxima_next and k == NG + 1:
                        negate_maxima(b + 1)
                    if k == COMB:
                        combine_heads()
                    if maxima_next and k == COMB + 1:
                        hand_over(b + 1)
                    if k == ATTN:
                        residual()
                        variance(link, x1, var2_done)
                    if k == NORM:
                        dve.wait_ge(rstd2_done, b + 1)
                        normalise(link, x1, attn, h2_nat, row(mod_post, 1), row(mod_post, 2), h2_done)
                    if k == ROUTE + 1:
                        rank_groups()
                    if k == ROUTE + 2:
                        choose_experts()
                    if k == ROUTE + 3:
                        weigh_experts()
                    if k >= WEIGHTS:
                        expert_block(k - WEIGHTS)
                dve.wait_ge(y_turned, b + 1)
                dve.tensor_tensor(y, bank[6].rearrange("p (n d) -> p n d", d=D), row(mod_post, 3),
                                  ALU.mult).then_inc(y_done, 1)
                dve.wait_ge(y_done, b + 1)
                dve.tensor_tensor(x1[:], y, x1[:], ALU.add).then_inc(x2_done, 1)
                if count != OUT_LINKS:
                    raise ValueError(f"OUT_LINKS is {count}")

            prepare(0)
            hand_over(0)
            for g in range(NG):
                group_halves(0, g)
                if g >= 1:
                    group_reduce(0, g - 1)
            group_reduce(0, NG - 1)
            negate_maxima(0)
            with dve.Fori(0, B - 1) as t:
                prepare(t + 1)
                after_attend(t, True)
            after_attend(B - 1, False)

        @block.tensor
        def _(pe):
            pe.wait_ge(weights_in, ALL_WEIGHTS)
            pe.wait_ge(silu_c_done, 1)
            for half in range(2):
                last = pe.matmul(ps[0:B, half, 0:3 * D], silu_c, wmod[:, 3 * D * half:3 * D * (half + 1)],
                                 start=True, stop=True)
            last.then_inc(mod_mm, 1)
            pe.wait_ge(consts_ready, 5)
            pe.wait_ge(vec_set, 3)

            def turn(dst, src, identity):
                for n in range(KB):
                    last = pe.transpose(dst(n), src(n), identity)
                return last

            def cut(tile, n):
                return tile[:, P * n:P * (n + 1)]

            def turn_h(b):
                pe.wait_ge(h_done, ONE + b + 1)
                turn(lambda n: cut(bank[3], n), lambda n: h_nat[:, n, :], ident[:]).then_inc(h_turned, 1)

            def project(b, w, before, done):
                pe.wait_ge(before, b + 1)
                pe.matmul(bank[3], w[:], h_t[:], start=True, stop=True).then_inc(done, 1)

            def project_v(b):
                pe.wait_ge(k_biased, b + 1)
                for n in range(KB):
                    last = pe.matmul(cut(bank[3], n), cut(h_t, n), wv[:], start=True, stop=True)
                last.then_inc(v_mm, 1)

            def linear_half(b, half):
                if half == 0:
                    pe.wait_ge(sigma_done, ONE + b + 1)
                    pe.nop(nofuse=True)
                    pe.wait_ge(v_new_done, b + 1)
                else:
                    pe.wait_ge(linear_halves, ONE + 2 * b + 1)
                for n in range(2):
                    last = pe.matmul(ps[:, 3, (D + H) * n:(D + H) * (n + 1)], cut(sigma, 2 * half + n), mz[:],
                                     start=True, stop=True)
                last.then_inc(linear_mm, 1)

            def lead_scores(b, g):
                pe.wait_ge(operands_a, ONE + 2 * NG * b + 2 * g + 2)
                for kb in range(KB):
                    n = KB * g + kb
                    dst = bank[n % NT]
                    if n >= NT:
                        m = n - NT
                        if m % 2 == 0:
                            pe.wait_ge(scores_copied, 2 * NG * b + 2 * (m // KB) + m % KB // 2 + 1)
                        else:
                            pe.wait_ge(half_maxima, ONE + 2 * NG * b + 2 * (m // KB) + m % KB // 2 + 1)
                    else:
                        pe.wait_ge(exps, ONE + KB * NG * b)
                    keys = k_pc if near(kb, g) else far_pc
                    last = pe.matmul(dst, cut(keys[:, 0, :], kb), content_op[:, g % 2, :], start=True,
                                     stop=not near(kb, g), skip_group_check=True)
                    for u in range(2 if near(kb, g) else 0):
                        t0 = P * kb - (QG * g + H * u) + S - 1
                        last = pe.matmul(dst.rearrange("p (h q) -> p h q", q=QG)[:, :, H * u:H * (u + 1)],
                                         rel_lead[:, t0:t0 + P], rel_op[:, g % 2, 256 * u:256 * (u + 1)],
                                         start=False, stop=(u == 1), skip_group_check=True)
                    last.then_inc(scores_a, 1)

            def turn_maxima(b, g):
                if g == 0:
                    pe.wait_ge(linear_halves, ONE + 2 * (b + 1))
                else:
                    pe.wait_ge(group_maxima, NG * b + g)
                pe.wait_ge(key_maxima, NG * b + g + 1)
                turn(lambda c: cut(bank[3].bitcast(BF16), c), lambda c: cut(key_max[:, g % 2, :], c),
                     identb[:]).then_inc(max_turned, 1)

            def turn_col_max(b):
                pe.wait_ge(group_maxima, NG * (b + 1))
                pe.nop(nofuse=True)
                pe.transpose(bank[3].bitcast(BF16)[0:KB * NG, 0:P], col_max[:].rearrange("p c g -> p (c g)"),
                             identb[:]).then_inc(col_max_turned, 1)

            def full_scores(b, n):
                kb, g = n // NG, n % NG
                dst = bank[n % NT]
                if n >= NT:
                    pe.wait_ge(exps, ONE + KB * NG * b + n - NT + 1)
                keys = kst if near(kb, g) else kst_far
                for hp in range(HP):
                    last = pe.matmul(dst[:, 2 * QG * hp:2 * QG * (hp + 1)], cut(keys[:, hp, :], kb),
                                     qst[:, hp, :, QG * g:QG * (g + 1)], start=(hp == 0),
                                     stop=(hp == HP - 1 and not near(kb, g)), skip_group_check=True)
                by_query = dst.rearrange("p (h q) -> p h q", q=QG)
                for j in range(0, QG if near(kb, g) else 0, 2):
                    q0 = QG * g + j
                    t0 = P * kb - q0 + S - 1
                    last = pe.matmul(by_query[:, :, j:j + 2], rel[:, t0:t0 + P], qrel[:, :, q0:q0 + 2],
                                     start=False, stop=(j == QG - 2), skip_group_check=True)
                last.then_inc(scores_b, 1)

            def values(b, u):
                kb, half = u // 2, u % 2
                if u == 0:
                    pe.wait_ge(handed_over, ONE + 2 * b + 2)
                    pe.nop(nofuse=True)
                    pe.wait_ge(x2_done, ONE + b)
                    pe.nop(nofuse=True)
                pe.wait_ge(exps, ONE + KB * NG * b + UNIT * (u + 1))
                for c in range(4):
                    for j in range(4):
                        last = pe.matmul(ps[32 * j:32 * (j + 1), 4 + c, QU * half:QU * (half + 1)],
                                         v_ones[:, kb, 4 * c + j, :], probs[:, u % 2, 4 * c + j, :],
                                         start=(u == 0), stop=(kb == KB - 1), tile_position=(0, 32 * j),
                                         skip_group_check=True)
                last.then_inc(pv_done, 1)

            def attend(b, prepare_next):
                pe.wait_ge(stacks_in, ONE + 16 * N_STACK * (b + 1))
                pe.nop(nofuse=True)
                pe.wait_ge(max_in, ONE + 16 * N_MAX * (b + 1))
                for n in range(KB * NG):
                    full_scores(b, n)
                    if n % UNIT == 2 and n >= UNIT:
                        values(b, n // UNIT - 1)
                    if prepare_next and n == TURN_H:
                        turn_h(b + 1)
                    if prepare_next and n == MM_Q:
                        project(b + 1, wq, h_t_done, q_mm)
                    if prepare_next and n == MM_K:
                        project(b + 1, wk, q_biased, k_mm)
                    if prepare_next and n == MM_V:
                        project_v(b + 1)
                    if prepare_next and n == MM_LIN0:
                        linear_half(b + 1, 0)
                    if prepare_next and n == MM_LIN1:
                        linear_half(b + 1, 1)
                values(b, NU - 1)

            def after_attend(b, maxima_next):
                def down(n):
                    if n < BLK:
                        pe.wait_ge(inner_done, BLK * b + n + 1)
                    else:
                        pe.wait_ge(gated_done, ONE + (BLK + 1) * (b + 1))
                    pe.matmul(bank[7], wd[:, n, :], inner[:, n % 2, :], start=(n == 0),
                              stop=(n == BLK)).then_inc(down_mm, 1)

                for k in range(SLOTS):
                    if maxima_next and k < NG:
                        lead_scores(b + 1, k)
                    if k == COMB:
                        pe.wait_ge(ctx_copied_a, 2 * b + 2)
                        pe.wait_ge(ctx_copied_v, 2 * b + 2)
                        for n in range(KB):
                            for c in range(4):
                                last = pe.transpose(cut(bank[4 + n], c), cut(ctx_t[:, c, :], n), ident[:])
                        last.then_inc(ctx_turned, 1)
                    if k == COMB + 1:
                        pe.wait_ge(comb_done, ONE + b + 1)
                        turn(lambda n: cut(bank[4], n), lambda n: comb[:, n, :], ident[:]).then_inc(comb_turned, 1)
                    if k == ATTN:
                        pe.wait_ge(comb_t_done, b + 1)
                        for n in range(KB):
                            last = pe.matmul(cut(bank[5], n), cut(comb_t, n), wo[:], start=True, stop=True)
                        last.then_inc(attn_mm, 1)
                    if k == TURN_H2:
                        pe.wait_ge(h2_done, b + 1)
                        turn(lambda n: cut(bank[6], n), lambda n: h2_nat[:, n, :], ident[:]).then_inc(h2_turned, 1)
                    if k == ROUTE:
                        pe.wait_ge(h2_t_done, b + 1)
                        for n in range(KB):
                            last = pe.matmul(ps[:, 7, E * n:E * (n + 1)], cut(h2_t, n), w_router[:],
                                             start=True, stop=True)
                        last.then_inc(logits_done, 1)
                    if k == WEIGHTS:
                        pe.wait_ge(combine_done, b + 1)
                        turn(lambda n: bank[6].bitcast(BF16)[0:3 * E, P * n:P * (n + 1)],
                             lambda n: combine_pc[:, n, :, :].rearrange("p s e -> p (s e)"),
                             identb[:]).then_inc(combine_turned, 1)
                    if maxima_next and 1 <= k <= NG:
                        turn_maxima(b + 1, k - 1)
                    if maxima_next and k == NG + 1:
                        turn_col_max(b + 1)
                    if k >= WEIGHTS:
                        n = k - WEIGHTS
                        if n >= 1:
                            pe.wait_ge(silu_done, (BLK + 1) * b + n)
                        pe.matmul(bank[4], wg[:, n, :], h2_t[:], start=True, stop=True).then_inc(gate_mm, 1)
                        if n >= 1:
                            pe.wait_ge(gated_done, ONE + (BLK + 1) * b + n)
                        pe.matmul(bank[5], wu[:, n, :], h2_t[:], start=True, stop=True).then_inc(up_mm, 1)
                        if n < BLK:
                            if n == 0:
                                pe.wait_ge(combine_t_done, b + 1)
                            else:
                                pe.wait_ge(inner_done, BLK * b + n)
                            pe.matmul(bank[6], sel[:, 2 * n:2 * n + 2, :].rearrange("p e i -> p (e i)"), combine_t[:],
                                      start=True, stop=True).then_inc(spread_mm, 1)
                        if n >= 1:
                            down(n - 1)
                down(BLK)
                pe.wait_ge(y_t_done, b + 1)
                turn(lambda n: cut(bank[6], n), lambda n: cut(y_t, n), ident[:]).then_inc(y_turned, 1)

            turn_h(0)
            project(0, wq, h_t_done, q_mm)
            project(0, wk, q_biased, k_mm)
            project_v(0)
            linear_half(0, 0)
            linear_half(0, 1)
            for g in range(NG):
                lead_scores(0, g)
                if g >= 1:
                    turn_maxima(0, g - 1)
            turn_maxima(0, NG - 1)
            turn_col_max(0)
            with pe.Fori(0, B - 1) as t:
                attend(t, True)
                after_attend(t, True)
            attend(B - 1, False)
            after_attend(B - 1, False)


def _layouts(v):
    f = np.float32
    t = lambda w: np.ascontiguousarray(np.asarray(w).T)
    by_dim = lambda w: np.asarray(w).reshape(H, HD, -1).transpose(1, 0, 2).reshape(D, -1)
    keys_of = np.clip(np.arange(2)[:, None] - (np.arange(TW) - (S - 1))[None, :], -MAX_REL, MAX_REL) + MAX_REL
    table = np.asarray(v["L0_attn_rel_emb"])[keys_of]
    rel = np.zeros((2, SLOT, TW), f)
    for r in range(len(PIECES)):
        rel[:, HD * r:HD * (r + 1)] = table.transpose(0, 2, 1)
    piece_mask = np.zeros((2, SLOT, 3), f)
    for r, (_, pk) in enumerate(PIECES):
        piece_mask[:, HD * r:HD * (r + 1), pk] = 1.0
    rel_lead = np.asarray(v["L0_attn_rel_emb"])[
        np.clip(np.arange(H)[:, None] - (np.arange(TW) - (S - 1))[None, :], -MAX_REL, MAX_REL) + MAX_REL]
    rel_far = np.stack([np.repeat(np.asarray(v["L0_attn_rel_emb"])[r], H) for r in (2 * MAX_REL, 0)], 1)
    mz = np.zeros((P, D + H), f)
    for h in range(H):
        mz[h::H, HD * h:HD * (h + 1)] = np.asarray(v["L0_attn_M"])[h]
        mz[h::H, D + h] = np.asarray(v["L0_attn_z"])[h]

    def inner_weights(routed, shared):
        w = np.concatenate([np.asarray(routed).reshape(E * I, D), np.asarray(shared)], 0)
        return np.ascontiguousarray(w.T).reshape(D, BLK + 1, P)

    down = np.asarray(v["L0_ffn_w_down"]).transpose(0, 2, 1).reshape(BLK, P, D)
    down = np.concatenate([down, t(v["L0_ffn_sh_down"])[None]], 0).transpose(1, 0, 2)
    return {
        "x": np.asarray(v["L0_attn_hidden_states"]), "c": t(v["L0_c"]),
        "rel_lead": np.ascontiguousarray(rel_lead.transpose(2, 0, 1)).reshape(P, TW), "rel_far": rel_far,
        "own": np.tile(np.eye(H, dtype=f), (HD, 1)),
        "ident": np.eye(P, dtype=f), "wq": t(by_dim(v["L0_attn_Wq"])), "wk": t(by_dim(v["L0_attn_Wk"])),
        "wv": t(v["L0_attn_Wv"]), "wo": t(v["L0_attn_Wo"]),
        "bq": by_dim(v["L0_attn_bq"]).reshape(P, 1), "bk": by_dim(v["L0_attn_bk"]).reshape(P, 1),
        "bv": np.asarray(v["L0_attn_bv"]), "bo": np.asarray(v["L0_attn_bo"]),
        "wmod": np.asarray(v["L0_wmod"]), "mz": mz,
        "gate_alpha": np.asarray(v["L0_attn_gate_alpha"]).reshape(1), "rel": rel.reshape(P, TW),
        "piece_mask": piece_mask.reshape(P, 3), "w_router": t(v["L0_ffn_gate_w"]),
        "b_router": np.asarray(v["L0_ffn_gate_bias"]),
        "wg": inner_weights(v["L0_ffn_w_gate"], v["L0_ffn_sh_gate"]),
        "wu": inner_weights(v["L0_ffn_w_up"], v["L0_ffn_sh_up"]),
        "wd": np.ascontiguousarray(down),
        "sel": np.tile(np.eye(E, dtype=f), (3, 1)),
    }


def kernel(**inputs):
    import concourse.bacc as bacc
    from concourse.bass_utils import run_bass_kernel_spmd

    nc = bacc.Bacc("TRN2", target_bir_lowering=False, num_devices=1)
    arrays, aps = {}, {}
    for name, value in _layouts(inputs).items():
        value = np.ascontiguousarray(value)
        arrays[f"in_{name}"] = value
        aps[name] = nc.dram_tensor(f"in_{name}", value.shape, mybir.dt.from_np(value.dtype),
                                   kind="ExternalInput").ap()
    out = nc.dram_tensor("out", (B, S, D), F32, kind="ExternalOutput").ap()
    build(nc, aps, out)
    result = run_bass_kernel_spmd(nc, [arrays], core_ids=[0])
    return result.results[0]["out"]
```

```python
from contextlib import ExitStack

import numpy as np

import concourse.bass as bass
from concourse import mybir

F32 = mybir.dt.float32
BF16 = mybir.dt.bfloat16
F32R = mybir.dt.float32r
ALU = mybir.AluOpType
ACT = mybir.ActivationFunctionType
AX_X = mybir.AxisListType.X

P = 128
B, S, D = 8, 512, 128
H, HD = 16, 8
HP = H // 2
KB = S // P
QG = 32
NG = S // QG
MAX_REL = 128
SLOT = 64
PIECES = [(0, 0), (0, 1), (0, 2), (1, 0), (1, 1), (2, 0)]
MROW = HD * len(PIECES)
TW = 2 * S
E, I, G = 32, 64, 8
TOPG, TOPK = 4, 8
BLK = E * I // P
BIG = 3.0e38
SCORE_SCALE = float(1.0 / np.sqrt(np.float32(HD)))

NT = 3
UNIT = 8
NU = KB * NG // UNIT
QU = QG * UNIT
NGATED = 6
NCOPY = 2
ONE = 1
PREP_LINKS, OUT_LINKS = 18, 27


def near(kb, g):
    return abs(kb - g * QG // P) <= 1


def build(nc, a, out):
    ctx = ExitStack()
    with ctx:
        def sb(name, shape, dt=F32):
            return ctx.enter_context(nc.sbuf_tensor(name, shape, dt))

        def sem(name):
            return ctx.enter_context(nc.semaphore(name))

        ident = sb("ident", [P, P])
        identb = sb("identb", [P, P], BF16)
        wq, wk, wv, wo = (sb(n, [P, D]) for n in ("wq", "wk", "wv", "wo"))
        bq, bk = sb("bq", [P, 1]), sb("bk", [P, 1])
        bv, bo = sb("bv", [P, D]), sb("bo", [P, 1])
        mod_all = sb("mod_all", [P, 7, B])
        mod_mag = sb("mod_mag", [P, 2, B])
        mz = sb("mz", [P, D + H])
        gate, one_minus_gate = sb("gate", [P, 1]), sb("one_minus_gate", [P, 1])
        gate_in = sb("gate_in", [P, 1])
        minus_half = sb("minus_half", [P, KB])
        rel = sb("rel", [P, TW], BF16)
        rel_lead = sb("rel_lead", [P, TW], BF16)
        rel_far = sb("rel_far", [P, 2])
        own = sb("own", [P, H])
        ownb = sb("ownb", [P, H], BF16)
        piece_mask = sb("piece_mask", [P, 3])
        w_router = sb("w_router", [P, E])
        b_router = sb("b_router", [P, E])
        wg_hi, wg_lo, wu_hi, wu_lo = (
            sb(n, [P, BLK + 1, P], F32R) for n in ("wg_hi", "wg_lo", "wu_hi", "wu_lo"))
        wd = sb("wd", [P, BLK + 1, P])
        sel32 = sb("sel32", [3 * E, E])
        sel = sb("sel", [3 * E, E, I], BF16)

        x_pre = sb("x_pre", [P, KB, D])
        mod_pre = sb("mod_pre", [P, 2])
        stats = sb("stats", [P, KB, 6])
        mean_var = sb("mean_var", [P, KB, 2])
        rstd = sb("rstd", [P, KB])
        h_t = sb("h_t", [P, S])
        q_t, k_t = sb("q_t", [P, S]), sb("k_t", [P, S])
        rest = sb("rest", [P, S])
        q_pc, k_pc, far_pc = (sb(n, [P, 3, S], BF16) for n in ("q_pc", "k_pc", "far_pc"))
        q_even, q_odd = sb("q_even", [P, 3, S], BF16), sb("q_odd", [P, 3, S], BF16)
        q_lead = sb("q_lead", [P, H, 2 * NG], BF16)
        sigma = sb("sigma", [P, S])
        v_new = sb("v_new", [P, KB, D])
        linear_new = sb("linear_new", [P, KB, D])
        linear_den = sb("linear_den", [P, KB, H])

        lead = sb("lead", [P, H, 2 * NG], BF16)
        content_op = sb("content_op", [P, 2, S], BF16)
        rel_op = sb("rel_op", [P, 2, S], BF16)
        copied = sb("copied", [P, NCOPY, KB, S], BF16)
        key_max = sb("key_max", [P, NCOPY, S], BF16)
        col_max = sb("col_max", [P, KB, NG], BF16)
        max_rows = sb("max_rows", [KB * NG, P], BF16)

        v_ones = sb("v_ones", [P, KB, H, 32])
        kst = sb("kst", [P, HP, S], BF16)
        kst_far = sb("kst_far", [P, HP, S], BF16)
        qst = sb("qst", [P, HP, 2, S], BF16)
        qrel = sb("qrel", [P, H, S], BF16)
        probs = sb("probs", [P, 2, H, QU])

        spare = probs[:].rearrange("p a h q -> p (a h q)")
        ctx_t = spare[:, 0:4 * S].rearrange("p (a q) -> p a q", a=4)
        comb = spare[:, 4 * S:5 * S].rearrange("p (n d) -> p n d", d=D)
        comb_t = spare[:, 5 * S:6 * S]
        gated = spare[:, 0:NGATED * S].rearrange("p (a q) -> p a q", a=NGATED)
        silu_g = spare[:, 6 * S:8 * S].rearrange("p (a q) -> p a q", a=2)
        inner = spare[:, 10 * S:12 * S].rearrange("p (a q) -> p a q", a=2)
        attn_t, y_t = spare[:, 8 * S:9 * S], spare[:, 9 * S:10 * S]
        h2_nat = spare[:, 12 * S:13 * S].rearrange("p (n d) -> p n d", d=D)
        h2_t = spare[:, 13 * S:14 * S]
        x_res = spare[:, 14 * S:15 * S].rearrange("p (n d) -> p n d", d=D)
        combine_t = spare[0:3 * E, 15 * S:15 * S + S // 2].bitcast(BF16)
        h2_hi, h2_lo = sb("h2_hi", [P, S], F32R), sb("h2_lo", [P, S], F32R)
        mod_post = sb("mod_post", [P, 5])
        linear = sb("linear", [P, KB, D])
        den_inv = sb("den_inv", [P, KB * H])
        x1 = sb("x1", [P, KB, D])
        score = sb("score", [P, KB, E])
        biased = sb("biased", [P, KB, E])
        pair_hi, pair_lo = sb("pair_hi", [P, KB * G, 2]), sb("pair_lo", [P, KB * G, 2])
        top1, top2 = sb("top1", [P, KB * G]), sb("top2", [P, KB * G])
        low_hi, hi_lo = sb("low_hi", [P, KB * G]), sb("hi_lo", [P, KB * G])
        group_sum = sb("group_sum", [P, KB, G + 4])
        group_top = sb("group_top", [P, KB, 8])
        group_left = sb("group_left", [P, KB, G + 4])
        group_mask = sb("group_mask", [P, KB, G])
        masked = sb("masked", [P, KB, E])
        expert_top = sb("expert_top", [P, KB, 8])
        expert_left = sb("expert_left", [P, KB, E])
        chosen = sb("chosen", [P, KB, E])
        weight = sb("weight", [P, KB, E])
        weight_sum = sb("weight_sum", [P, KB])
        combine = sb("combine", [P, KB, E])
        combine_rest = sb("combine_rest", [P, KB, E])
        combine_pc = sb("combine_pc", [P, KB, 3, E], BF16)

        rel32 = spare[:, 0:TW]
        rel_lead32 = spare[:, TW:2 * TW]
        wmod = spare[:, 2 * TW:2 * TW + 6 * D]
        c_t = spare[:, 2 * TW + 6 * D:2 * TW + 6 * D + B]
        silu_c = spare[:, 2 * TW + 6 * D + B:2 * TW + 6 * D + 2 * B]
        rel_rest = rel_lead32
        rel_piece = wmod[:, 0:TW // 2].bitcast(BF16)
        wg32, wu32 = (spare[:, 3 * TW + n * (BLK + 1) * P:3 * TW + (n + 1) * (BLK + 1) * P].rearrange(
            "p (n i) -> p n i", i=P) for n in range(2))

        ps = ctx.enter_context(nc.psum_tensor("ps", [P, 8, 512], F32))
        bank = [ps[:, n, :] for n in range(8)]

        k_dram = nc.dram_tensor("k_pieces", [2, 3, D, S], BF16, kind="Internal").ap()
        q_dram = nc.dram_tensor("q_pieces", [3, 3, D, S], BF16, kind="Internal").ap()
        max_dram = nc.dram_tensor("max_rows_by_slot", [2, HP, NG, QG], BF16, kind="Internal").ap()
        lead_dram = nc.dram_tensor("q_lead_rows", [H, D, 2 * NG], BF16, kind="Internal").ap()

        mod_in, experts_hi = sem("mod_in"), sem("experts_hi")
        first_in, tables_in, experts_in = sem("first_in"), sem("tables_in"), sem("experts_in")
        pool_set, vec_set, masks_ready, rel_lead_ready = (
            sem(n) for n in ("pool_set", "vec_set", "masks_ready", "rel_lead_ready"))
        consts_chain, consts_ready = sem("consts_chain"), sem("consts_ready")
        silu_c_done, gate_act, mod_mm = sem("silu_c_done"), sem("gate_act"), sem("mod_mm")
        lead_copied, lead_stored, max_stored = sem("lead_copied"), sem("lead_stored"), sem("max_stored")
        x_in, var_done, rstd_done, h_done, h_turned, h_t_done = (
            sem(n) for n in ("x_in", "var_done", "rstd_done", "h_done", "h_turned", "h_t_done"))
        q_mm, k_mm, v_mm, q_biased, k_biased, v_new_done = (
            sem(n) for n in ("q_mm", "k_mm", "v_mm", "q_biased", "k_biased", "v_new_done"))
        q_pieces_done, k_pieces_done, far_pieces_done, q_copies_done = (
            sem(n) for n in ("q_pieces_done", "k_pieces_done", "far_pieces_done", "q_copies_done"))
        pieces_stored, lead_in, stacks_in = sem("pieces_stored"), sem("lead_in"), sem("stacks_in")
        neg_part_done, neg_exp_done, sigma_done, linear_mm, linear_halves = (
            sem(n) for n in ("neg_part_done", "neg_exp_done", "sigma_done", "linear_mm", "linear_halves"))
        prep_chain, out_chain = sem("prep_chain"), sem("out_chain")
        operands_a, scores_a, scores_copied, half_maxima, key_maxima = (
            sem(n) for n in ("operands_a", "scores_a", "scores_copied", "half_maxima", "key_maxima"))
        max_turned, group_maxima, col_max_turned, max_rows_done, max_in = (
            sem(n) for n in ("max_turned", "group_maxima", "col_max_turned", "max_rows_done", "max_in"))
        handed_over, scores_b, exps, pv_done = (sem(n) for n in ("handed_over", "scores_b", "exps", "pv_done"))
        res_in, ctx_copied_a, ctx_copied_v, ctx_turned = (
            sem(n) for n in ("res_in", "ctx_copied_a", "ctx_copied_v", "ctx_turned"))
        comb_done, comb_turned, comb_t_done, attn_mm, attn_t_done, attn_turned, residual_done = (
            sem(n) for n in ("comb_done", "comb_turned", "comb_t_done", "attn_mm", "attn_t_done", "attn_turned",
                             "residual_done"))
        var2_done, rstd2_done, h2_done, h2_turned, h2_t_done, h2_split = (
            sem(n) for n in ("var2_done", "rstd2_done", "h2_done", "h2_turned", "h2_t_done", "h2_split"))
        logits_done, sigmoid_done, combine_done, combine_turned, combine_t_done = (
            sem(n) for n in ("logits_done", "sigmoid_done", "combine_done", "combine_turned", "combine_t_done"))
        gate_mm, up_mm, spread_mm, silu_done, gated_done, inner_done, down_mm = (
            sem(n) for n in ("gate_mm", "up_mm", "spread_mm", "silu_done", "gated_done", "inner_done", "down_mm"))
        y_t_done, y_turned, x2_done, stored = (sem(n) for n in ("y_t_done", "y_turned", "x2_done", "stored"))
        carried = [h_done, x2_done, q_copies_done, stacks_in, operands_a, scores_b, pieces_stored, scores_a,
                   col_max_turned, max_in, exps, pv_done, comb_done, sigma_done, h_turned, far_pieces_done,
                   stored, linear_halves, linear_mm, handed_over, lead_copied, lead_stored,
                   max_stored]

        mod_loads = [(c_t, a["c"]), (wmod, a["wmod"]), (bo[:], a["bo"])]
        first_loads = [
            (ident[:], a["ident"]), (wq[:], a["wq"]), (wk[:], a["wk"]),
            (wv[:], a["wv"]), (bq[:], a["bq"]), (bk[:], a["bk"]), (bv[:], a["bv"].partition_broadcast(P)),
            (gate_in[:], a["gate_alpha"].partition_broadcast(P)), (mz[:], a["mz"]), (rel_far[:], a["rel_far"]),
            (own[:], a["own"]),
        ]
        table_loads = [
            (rel_lead32, a["rel_lead"]), (rel32, a["rel"]), (piece_mask[:], a["piece_mask"]), (wo[:], a["wo"]),
            (w_router[:], a["w_router"]),
            (b_router[:], a["b_router"].partition_broadcast(P)), (sel32[:], a["sel"]),
        ]
        expert_loads = [(wg32, a["wg"]), (wu32, a["wu"]), (wd[:], a["wd"])]
        N_STORES = 5
        RUNS = [(0, 3, 0, 0), (3, 2, 1, 0), (5, 1, 2, 0)]
        N_STACK = 2 * (len(PIECES) + 3 * len(RUNS))
        N_MAX = 2

        TURN_H, MM_Q, MM_K, MM_V, EXP_NEG, MM_LIN0, MM_LIN1 = 18, 21, 26, 34, 37, 42, 48
        PE_AT = dict(context=2, comb=6, attn=8, attn_turn=10, h2=15, route=18, weights=25)
        ACT_AT = dict(comb=6, attn=8, h2=15, route=18, weights=26)
        DVE_AT = dict(comb=4, hand=8, residual=10, norm=13, split=17, rank=19, choose=19, weigh=23)
        GATES, WEIGHTS = 9, 12
        SECOND_NORM = 7
        SLOTS = GATES + BLK + 2
        weighted_at = {k: [] for k in range(SLOTS)}
        for n in range(BLK + 1):
            k = max(WEIGHTS, GATES + n + 1)
            while len(weighted_at[k]) == 2:
                k += 1
            weighted_at[k].append(n)
        VALUES = (1, 3, 5, 7)
        POOL_SETS, VEC_SETS = 6, 4
        LAG = 2

        block = ctx.enter_context(nc.Block())

        @block.sync
        def _(sp):
            def load(pairs, done):
                for dst, src in pairs:
                    sp.dma_start(dst, src).then_inc(done, 16)

            def load_x(b):
                sp.dma_start(x_pre[:], a["x"][bass.ds(b, 1)].rearrange("o (n p) d -> p (o n) d", p=P)
                             ).then_inc(x_in, 16)

            def load_for_output(b):
                sp.wait_ge(pv_done, ONE + NU * (b + 1))
                sp.nop(nofuse=True)
                sp.dma_start(x_res, a["x"][bass.ds(b, 1)].rearrange("o (n p) d -> p (o n) d", p=P)).then_inc(res_in, 16)

            def store_pieces(b):
                sp.wait_ge(stacks_in, ONE + 16 * N_STACK * b)
                sp.nop(nofuse=True)
                sp.wait_ge(lead_copied, ONE + b + 1)
                sp.dma_start(lead_dram.rearrange("i p j -> p i j"), q_lead[:]).then_inc(lead_stored, 16)
                sp.wait_ge(q_pieces_done, b + 1)
                sp.dma_start(q_dram[0].rearrange("r p q -> p r q"), q_pc[:]).then_inc(pieces_stored, 16)
                sp.wait_ge(k_pieces_done, b + 1)
                sp.dma_start(k_dram[0].rearrange("r p q -> p r q"), k_pc[:]).then_inc(pieces_stored, 16)
                sp.wait_ge(lead_stored, ONE + 16 * (b + 1))
                sp.nop(nofuse=True)
                sp.wait_ge(operands_a, ONE + 2 * NG * b)
                sp.dma_start(lead[:].rearrange("p h j -> p (h j)"),
                             lead_dram.rearrange("i (d h) j -> d i (h j)", d=HD)).then_inc(lead_in, 16)
                sp.wait_ge(q_copies_done, ONE + 2 * b + 2)
                sp.dma_start(q_dram[1].rearrange("r p q -> p r q"), q_even[:]).then_inc(pieces_stored, 16)
                sp.dma_start(q_dram[2].rearrange("r p q -> p r q"), q_odd[:]).then_inc(pieces_stored, 16)
                sp.wait_ge(far_pieces_done, ONE + b + 1)
                sp.dma_start(k_dram[1].rearrange("r p q -> p r q"), far_pc[:]).then_inc(pieces_stored, 16)

            def load_stacks(b):
                sp.wait_ge(pieces_stored, ONE + 16 * N_STORES * (b + 1))
                sp.nop(nofuse=True)
                sp.wait_ge(scores_b, ONE + KB * NG * b)
                for s in range(2):
                    for r, (pq, _) in enumerate(PIECES):
                        rows = slice(SLOT * s + HD * r, SLOT * s + HD * (r + 1))
                        sp.dma_start(qst[rows, :, s, :], q_dram[0, pq].rearrange("(d a s) q -> s d a q", d=HD, s=2)[s]
                                     ).then_inc(stacks_in, 16)
                    for r, n, pq, pk in RUNS:
                        rows = slice(SLOT * s + HD * r, SLOT * s + HD * (r + n))
                        for dst, keys in ((kst, k_dram[0]), (kst_far, k_dram[1])):
                            sp.dma_start(dst[rows], keys[pk:pk + n].rearrange("r (d a s) q -> s (r d) a q", d=HD, s=2)[s]
                                         ).then_inc(stacks_in, 16)
                        sp.dma_start(qrel[rows].rearrange("p h q -> p (h q)"),
                                     q_dram[1 + s, pq].rearrange("(d h) q -> d (h q)", d=HD).unsqueeze(0).broadcast_to(
                                         [n, HD, H * S])).then_inc(stacks_in, 16)

            def load_maxima(b):
                sp.wait_ge(max_in, ONE + 32 * b)
                sp.nop(nofuse=True)
                sp.wait_ge(max_rows_done, b + 1)
                for a2 in range(2):
                    for s in range(2):
                        sp.dma_start(max_dram[s].rearrange("(c a) g q -> a c g q", a=2)[a2],
                                     max_rows[:, (2 * a2 + s) * QG:(2 * a2 + s + 1) * QG]).then_inc(max_stored, 16)
                sp.wait_ge(max_stored, ONE + 64 * (b + 1))
                sp.nop(nofuse=True)
                for s in range(2):
                    sp.dma_start(qst[SLOT * s + MROW:SLOT * s + MROW + 1, :, s, :],
                                 max_dram[s:s + 1].rearrange("s a g q -> s a (g q)")).then_inc(max_in, 16)

            def store_out(b):
                sp.wait_ge(x2_done, ONE + b + 1)
                sp.nop(nofuse=True)
                sp.dma_start(out[bass.ds(b, 1)].rearrange("o (n p) d -> p (o n) d", p=P), x1[:]).then_inc(stored, 16)

            load(mod_loads, mod_in)
            load_x(0)
            load(first_loads, first_in)
            load(table_loads, tables_in)
            load(expert_loads, experts_in)
            store_pieces(0)
            sp.wait_ge(pool_set, POOL_SETS)
            sp.wait_ge(vec_set, VEC_SETS)
            load_stacks(0)
            load_maxima(0)
            with sp.Fori(0, B - 1) as t:
                sp.wait_ge(h_turned, ONE + t + 1)
                sp.nop(nofuse=True)
                load_x(t + 1)
                store_pieces(t + 1)
                load_for_output(t)
                load_stacks(t + 1)
                load_maxima(t + 1)
                store_out(t)
            load_for_output(B - 1)
            store_out(B - 1)
            sp.wait_ge(stored, ONE + 16 * B)

        @block.gpsimd
        def _(pool):
            for s in carried:
                pool.sem_inc(s, ONE)
            pool.memset(minus_half[:], -0.5).then_inc(pool_set, 1)
            pool.memset(q_even[:], 0.0).then_inc(pool_set, 1)
            pool.memset(q_odd[:], 0.0).then_inc(pool_set, 1)

            def first_norm(b):
                pool.wait_ge(var_done, b + 1)
                pool.tensor_tensor(rstd[:], mean_var[:, :, 1], minus_half[:], ALU.pow).then_inc(rstd_done, 1)

            def query_copies(b):
                pool.wait_ge(q_pieces_done, b + 1)
                pool.nop(nofuse=True)
                pool.wait_ge(pieces_stored, ONE + 16 * N_STORES * b)
                pool.nop(nofuse=True)
                for parity, dst in enumerate((q_even, q_odd)):
                    pool.tensor_copy(dst[:, :, parity:S:2], q_pc[:, :, parity:S:2]).then_inc(q_copies_done, 1)

            def group_operands(b, g):
                if g == 0:
                    pool.wait_ge(lead_in, 16 * (b + 1))
                    pool.nop(nofuse=True)
                pool.wait_ge(scores_a, ONE + KB * NG * b + KB * max(g - 1, 0))
                pool.tensor_tensor(content_op[:, g % 2, :].rearrange("p (h q) -> p h q", q=QG),
                                   q_pc[:, 0, QG * g:QG * (g + 1)].unsqueeze(1).broadcast_to([P, H, QG]),
                                   ownb[:].unsqueeze(2).broadcast_to([P, H, QG]), ALU.mult).then_inc(operands_a, 1)
                for u in range(2):
                    last = pool.tensor_tensor(rel_op[:, g % 2, 256 * u:256 * (u + 1)].rearrange("p (h i) -> p h i", i=H),
                                              lead[:, :, 2 * g + u:2 * g + u + 1].broadcast_to([P, H, H]),
                                              ownb[:].unsqueeze(1).broadcast_to([P, H, H]), ALU.mult)
                last.then_inc(operands_a, 1)

            def second_norm(b):
                pool.wait_ge(var2_done, b + 1)
                pool.tensor_tensor(rstd[:], mean_var[:, :, 1], minus_half[:], ALU.pow).then_inc(rstd2_done, 1)

            pool.wait_ge(pool_set, 1)
            first_norm(0)
            pool.memset(kst[:], 1.0).then_inc(pool_set, 1)
            pool.memset(kst_far[:], 1.0).then_inc(pool_set, 1)
            pool.memset(qst[:], 0.0).then_inc(pool_set, 1)
            pool.wait_ge(pool_set, POOL_SETS)
            query_copies(0)
            pool.wait_ge(masks_ready, 1)
            for g in range(NG):
                group_operands(0, g)
            pool.wait_ge(experts_hi, 1)
            pool.tensor_tensor(wg_lo[:], wg32, wg_hi[:], ALU.subtract).then_inc(consts_ready, 1)
            pool.wait_ge(experts_hi, 2)
            pool.tensor_tensor(wu_lo[:], wu32, wu_hi[:], ALU.subtract).then_inc(consts_ready, 1)
            with pool.Fori(0, B - 1) as t:
                first_norm(t + 1)
                query_copies(t + 1)
                for g in range(NG):
                    group_operands(t + 1, g)
                    if g == SECOND_NORM:
                        second_norm(t)
            second_norm(B - 1)

        @block.scalar
        def _(act):
            act.wait_ge(mod_in, 16 * len(mod_loads))
            act.activation(silu_c, c_t, ACT.Silu).then_inc(silu_c_done, 1)
            act.wait_ge(first_in, 16 * len(first_loads))
            act.activation(gate[:], gate_in[:], ACT.Sigmoid).then_inc(gate_act, 1)

            def turned_h(b):
                act.wait_ge(h_turned, ONE + b + 1)
                act.activation(h_t[:], bank[3], ACT.Identity, bias=mod_pre[:, 0:1],
                               scale=mod_pre[:, 1:2]).then_inc(h_t_done, 1)

            def bias_q(b):
                act.wait_ge(sigma_done, ONE + b)
                act.wait_ge(q_mm, b + 1)
                act.activation(q_t[:], bank[3], ACT.Identity, bias=bq[:]).then_inc(q_biased, 1)

            def bias_k(b):
                act.wait_ge(far_pieces_done, ONE + b)
                act.wait_ge(k_mm, b + 1)
                act.activation(k_t[:], bank[3], ACT.Identity, bias=bk[:]).then_inc(k_biased, 1)

            def copy_lead(b):
                act.wait_ge(q_pieces_done, b + 1)
                act.wait_ge(lead_stored, ONE + 16 * b)
                act.copy(q_lead[:], q_pc[:, 0, :].rearrange("p (j i) -> p i j", i=H)).then_inc(lead_copied, 1)

            def exp_negative(b):
                act.wait_ge(neg_part_done, b + 1)
                act.activation(sigma[:], sigma[:], ACT.Exp).then_inc(neg_exp_done, 1)

            def copy_scores(b, g):
                if g >= NCOPY:
                    act.wait_ge(key_maxima, NG * b + g - NCOPY + 1)
                for kb in range(KB):
                    act.wait_ge(scores_a, ONE + KB * NG * b + KB * g + kb + 1)
                    act.copy(copied[:, g % NCOPY, kb, :], bank[(KB * g + kb) % NT]).then_inc(scores_copied, 1)

            def attend(b, prepare_next):
                for n in range(KB * NG):
                    kb, g, u = n // NG, n % NG, n // UNIT
                    if n % UNIT == 0:
                        act.wait_ge(pv_done, ONE + NU * b + max(u - 1, 0))
                    act.wait_ge(scores_b, ONE + KB * NG * b + n + 1)
                    q0 = QG * (g % UNIT)
                    act.activation(probs[:, u % 2, :, q0:q0 + QG], bank[n % NT].rearrange("p (h q) -> p h q", q=QG),
                                   ACT.Exp, scale=SCORE_SCALE).then_inc(exps, 1)
                    if prepare_next and n == TURN_H:
                        turned_h(b + 1)
                    if prepare_next and n == MM_Q:
                        bias_q(b + 1)
                    if prepare_next and n == MM_K:
                        bias_k(b + 1)
                        copy_lead(b + 1)
                    if prepare_next and n == EXP_NEG:
                        exp_negative(b + 1)

            def after_attend(b, maxima_next):
                act.wait_ge(pv_done, ONE + NU * (b + 1))
                for c in range(2):
                    act.copy(ctx_t[:, c, :], bank[4 + c]).then_inc(ctx_copied_a, 1)

                def steps(h):
                    if h == ACT_AT["comb"]:
                        act.wait_ge(comb_turned, b + 1)
                        act.copy(comb_t, bank[4]).then_inc(comb_t_done, 1)
                    if h == ACT_AT["attn"]:
                        act.wait_ge(attn_mm, b + 1)
                        act.activation(attn_t, bank[5], ACT.Identity, bias=mod_post[:, 4:5],
                                       scale=mod_post[:, 0:1]).then_inc(attn_t_done, 1)
                    if h == ACT_AT["h2"]:
                        act.wait_ge(h2_turned, b + 1)
                        act.activation(h2_t, bank[6], ACT.Identity, bias=mod_post[:, 1:2],
                                       scale=mod_post[:, 2:3]).then_inc(h2_t_done, 1)
                    if h == ACT_AT["route"]:
                        act.wait_ge(logits_done, b + 1)
                        act.activation(score[:], ps[:, 7, 0:KB * E].rearrange("p (n e) -> p n e", e=E),
                                       ACT.Sigmoid).then_inc(sigmoid_done, 1)
                    if h == ACT_AT["weights"]:
                        act.wait_ge(combine_turned, b + 1)
                        act.copy(combine_t, bank[6].bitcast(BF16)[0:3 * E, 0:S]).then_inc(combine_t_done, 1)

                for k in range(SLOTS):
                    steps(2 * k)
                    if maxima_next and k < NG:
                        copy_scores(b + 1, k)
                    steps(2 * k + 1)
                    if GATES <= k <= GATES + BLK:
                        n = k - GATES
                        act.wait_ge(gate_mm, (BLK + 1) * b + n + 1)
                        if n >= 2:
                            act.wait_ge(gated_done, (BLK + 1) * b + n - 1)
                        act.activation(silu_g[:, n % 2, :], bank[4], ACT.Silu).then_inc(silu_done, 1)
                act.wait_ge(down_mm, (BLK + 1) * (b + 1))
                act.activation(y_t, bank[7], ACT.Identity, scale=mod_post[:, 3:4]).then_inc(y_t_done, 1)

            turned_h(0)
            bias_q(0)
            bias_k(0)
            copy_lead(0)
            exp_negative(0)
            for g in range(NG):
                copy_scores(0, g)
            act.wait_ge(experts_in, 16 * len(expert_loads))
            act.copy(wg_hi[:], wg32).then_inc(experts_hi, 1)
            act.copy(wu_hi[:], wu32).then_inc(experts_hi, 1)
            act.wait_ge(tables_in, 16 * len(table_loads))
            act.copy(sel[:], sel32[:].unsqueeze(2).broadcast_to([3 * E, E, I])).then_inc(consts_ready, 1)
            with act.Fori(0, B - 1) as t:
                attend(t, True)
                after_attend(t, True)
            attend(B - 1, False)
            after_attend(B - 1, False)

        @block.vector
        def _(dve):
            dve.memset(v_ones[:], 0.0).then_inc(vec_set, 1)
            dve.wait_ge(vec_set, 1)
            dve.memset(v_ones[:, :, :, HD:HD + 1], 1.0).then_inc(vec_set, 1)
            dve.memset(group_sum[:, :, G:G + 4], BIG).then_inc(vec_set, 1)
            consts = 0

            def const_link(ins):
                nonlocal consts
                consts += 1
                ins.then_inc(consts_chain, 1)
                dve.wait_ge(consts_chain, consts)

            scales, gates = mod_all[:, 1:5:3, :], mod_all[:, 2:6:3, :]
            dve.wait_ge(mod_mm, 1)
            const_link(dve.tensor_copy(mod_all[:, 0:6, :], ps[:, 0, 0:6 * B].rearrange("p (m b) -> p m b", b=B)))
            const_link(dve.tensor_scalar(scales, scales, 1.0, None, ALU.add))
            const_link(dve.tensor_scalar(mod_mag[:], gates, -1.0, 0.25, ALU.mult, ALU.max))
            const_link(dve.tensor_tensor(mod_mag[:], mod_mag[:], gates, ALU.max))
            const_link(dve.tensor_scalar(gates, gates, 0.0, 2.0, ALU.is_ge, ALU.mult))
            const_link(dve.scalar_tensor_tensor(gates, gates, 1.0, mod_mag[:], ALU.subtract, ALU.mult))
            const_link(dve.tensor_scalar(mod_all[:, 6, :], mod_all[:, 2, :], bo[:], None, ALU.mult))

            def cut_table():
                const_link(dve.tensor_copy(rel_piece, rel32))
                const_link(dve.tensor_scalar(rel[:], rel_piece, piece_mask[:, 0:1], None, ALU.mult))
                for piece in (1, 2):
                    left = rel32 if piece == 1 else rel_rest
                    const_link(dve.tensor_tensor(rel_rest, left, rel_piece, ALU.subtract))
                    const_link(dve.tensor_copy(rel_piece, rel_rest))
                    ins = dve.scalar_tensor_tensor(rel[:], rel_piece, piece_mask[:, piece:piece + 1], rel[:],
                                                   ALU.mult, ALU.add)
                    if piece == 1:
                        const_link(ins)
                ins.then_inc(consts_ready, 1)

            def variance(link, src, ready):
                for n in range(KB):
                    last = dve.bn_stats(stats[:, n, :], src[:, n, :])
                link(last)
                dve.nop(nofuse=True)
                for n in range(KB):
                    last = dve.bn_aggr(mean_var[:, n, :], stats[:, n, :])
                link(last)
                dve.tensor_scalar(mean_var[:, :, 1], mean_var[:, :, 1], 1e-5, None, ALU.add).then_inc(ready, 1)

            def normalise(src, to, done):
                for n in range(KB):
                    last = dve.tensor_scalar(to[:, n, :], src[:, n, :], mean_var[:, n, 0:1], rstd[:, n:n + 1],
                                             ALU.subtract, ALU.mult)
                last.then_inc(done, 1)

            def batch_columns(dst, first, count, b):
                dve.tensor_copy(dst[:], mod_all[:, first:first + count, bass.ds(b, 1)].rearrange("p m o -> p (m o)"))

            def prepare(b, first=False):
                count = 0

                def link(ins):
                    nonlocal count
                    count += 1
                    ins.then_inc(prep_chain, 1)
                    dve.wait_ge(prep_chain, PREP_LINKS * b + count)

                dve.wait_ge(x_in, 16 * (b + 1))
                variance(link, x_pre, var_done)
                dve.wait_ge(rstd_done, b + 1)
                dve.wait_ge(h_turned, ONE + b)
                batch_columns(mod_pre, 0, 2, b)
                normalise(x_pre, x_pre, h_done)
                if first:
                    dve.memset(qrel[:], 0.0).then_inc(vec_set, 1)
                    dve.wait_ge(first_in, 16 * len(first_loads))
                    dve.tensor_copy(ownb[:], own[:]).then_inc(masks_ready, 1)
                    dve.tensor_copy(identb[:], ident[:]).then_inc(masks_ready, 1)
                    dve.wait_ge(gate_act, 1)
                    dve.tensor_scalar(one_minus_gate[:], gate[:], -1.0, 1.0, ALU.mult, ALU.add).then_inc(masks_ready, 1)
                    dve.wait_ge(masks_ready, 3)

                def split(src, pc, done):
                    link(dve.tensor_copy(pc[:, 0, :], src[:]))
                    link(dve.tensor_tensor(rest[:], src[:], pc[:, 0, :], ALU.subtract))
                    link(dve.tensor_copy(pc[:, 1, :], rest[:]))
                    dve.tensor_tensor(pc[:, 2, :], rest[:], pc[:, 1, :], ALU.subtract).then_inc(done, 1)

                dve.wait_ge(pieces_stored, ONE + 16 * N_STORES * b)
                dve.wait_ge(q_copies_done, ONE + 2 * b)
                dve.wait_ge(lead_copied, ONE + b)
                dve.wait_ge(operands_a, ONE + 2 * NG * b)
                dve.wait_ge(q_biased, b + 1)
                split(q_t, q_pc, q_pieces_done)
                dve.wait_ge(linear_mm, ONE + 2 * b)
                dve.tensor_scalar(sigma[:], q_t[:], 0.0, None, ALU.min).then_inc(neg_part_done, 1)
                dve.wait_ge(q_pieces_done, b + 1)
                dve.wait_ge(scores_a, ONE + KB * NG * b)
                dve.wait_ge(k_biased, b + 1)
                split(k_t, k_pc, k_pieces_done)
                for far in range(2):
                    half = slice(far * S // 2, (far + 1) * S // 2)
                    last = dve.tensor_scalar(k_t[:, half], k_t[:, half], rel_far[:, far:far + 1], None, ALU.add)
                link(last)
                dve.wait_ge(k_pieces_done, b + 1)
                split(k_t, far_pc, far_pieces_done)
                dve.wait_ge(handed_over, ONE + 2 * b)
                dve.wait_ge(v_mm, b + 1)
                dve.tensor_tensor(v_new[:], bank[3].rearrange("p (n d) -> p n d", d=D),
                                  bv[:].unsqueeze(1).broadcast_to([P, KB, D]), ALU.add).then_inc(v_new_done, 1)
                dve.wait_ge(neg_exp_done, b + 1)
                dve.scalar_tensor_tensor(sigma[:], q_t[:], 0.0, sigma[:], ALU.max, ALU.add).then_inc(sigma_done, 1)
                for half in range(2):
                    dve.wait_ge(linear_mm, ONE + 2 * b + half + 1)
                    two = ps[:, 3, 0:2 * (D + H)].rearrange("p (n m) -> p n m", m=D + H)
                    den = linear_den[:, 2 * half:2 * half + 2, :]
                    link(dve.tensor_scalar(den, two[:, :, D:D + H], 1e-6, None, ALU.add))
                    link(dve.reciprocal(den, den))
                    link(dve.tensor_scalar(den, den, one_minus_gate[:], None, ALU.mult))
                    dve.tensor_tensor(
                        linear_new[:, 2 * half:2 * half + 2, :].rearrange("p n (h d) -> p n h d", d=HD),
                        two[:, :, 0:D].rearrange("p n (h d) -> p n h d", d=HD),
                        den.unsqueeze(3).broadcast_to([P, 2, H, HD]), ALU.mult).then_inc(linear_halves, 1)
                if count != PREP_LINKS:
                    raise ValueError(f"PREP_LINKS is {count}")

            def hand_over(b):
                dve.wait_ge(v_new_done, b + 1)
                dve.wait_ge(pv_done, ONE + NU * b)
                dve.tensor_copy(v_ones[:, :, :, 0:HD].rearrange("p n h d -> p (n h) d"),
                                v_new[:].rearrange("p n (h d) -> p (n h) d", d=HD)).then_inc(handed_over, 1)
                dve.wait_ge(linear_halves, ONE + 2 * (b + 1))
                dve.wait_ge(comb_done, ONE + b)
                dve.tensor_copy(linear[:], linear_new[:]).then_inc(handed_over, 1)

            def group_halves(b, g):
                half = copied[:, g % NCOPY]
                dve.wait_ge(scores_copied, KB * NG * b + KB * (g + 1))
                dve.tensor_tensor(half[:, 0:2, :], half[:, 0:2, :], half[:, 2:4, :], ALU.max).then_inc(half_maxima, 1)
                if g >= NCOPY:
                    dve.wait_ge(max_turned, NG * b + g - NCOPY + 1)
                dve.wait_ge(half_maxima, NG * b + g + 1)
                dve.tensor_tensor(key_max[:, g % NCOPY, :], half[:, 0, :], half[:, 1, :], ALU.max).then_inc(key_maxima, 1)

            def group_reduce(b, g):
                if g == 0:
                    dve.wait_ge(col_max_turned, ONE + b)
                dve.wait_ge(max_turned, NG * b + g + 1)
                dve.tensor_reduce(col_max[:, :, g], bank[3].bitcast(BF16)[:, 0:KB * P].rearrange(
                    "p (c k) -> p c k", k=P), AX_X, ALU.max).then_inc(group_maxima, 1)

            def negate_maxima(b):
                dve.wait_ge(max_stored, ONE + 64 * b)
                dve.wait_ge(col_max_turned, ONE + b + 1)
                dve.tensor_scalar(max_rows[:], bank[3].bitcast(BF16)[0:KB * NG, 0:P], -1.0, None,
                                  ALU.mult).then_inc(max_rows_done, 1)

            def after_attend(b, maxima_next):
                count = 0

                def link(ins):
                    nonlocal count
                    count += 1
                    ins.then_inc(out_chain, 1)
                    dve.wait_ge(out_chain, OUT_LINKS * b + count)

                def combine_heads():
                    dve.wait_ge(ctx_turned, b + 1)
                    local = ps[:, 4:8, :].rearrange("p n (h m) -> p (n h) m", m=32)
                    link(dve.reciprocal(den_inv[:], local[:, :, HD]))
                    link(dve.tensor_scalar(den_inv[:], den_inv[:], gate[:], None, ALU.mult))
                    link(dve.tensor_tensor(comb.rearrange("p n (h d) -> p (n h) d", d=HD), local[:, :, 0:HD],
                                           den_inv[:].unsqueeze(2).broadcast_to([P, KB * H, HD]), ALU.mult))
                    dve.tensor_tensor(comb, comb, linear[:], ALU.add).then_inc(comb_done, 1)

                def residual():
                    dve.wait_ge(res_in, 16 * (b + 1))
                    dve.wait_ge(stored, ONE + 16 * b)
                    dve.wait_ge(attn_turned, b + 1)
                    dve.tensor_tensor(x1[:], bank[5].rearrange("p (n d) -> p n d", d=D), x_res,
                                      ALU.add).then_inc(residual_done, 1)
                    dve.wait_ge(residual_done, b + 1)

                def rank_groups():
                    dve.wait_ge(sigmoid_done, b + 1)
                    link(dve.tensor_tensor(biased[:], score[:], b_router[:].unsqueeze(1).broadcast_to([P, KB, E]),
                                           ALU.add))
                    quads = biased[:].rearrange("p n (g j two) -> p (n g) j two", j=2, two=2)
                    dve.tensor_tensor(pair_hi[:], quads[:, :, :, 0], quads[:, :, :, 1], ALU.max)
                    link(dve.tensor_tensor(pair_lo[:], quads[:, :, :, 0], quads[:, :, :, 1], ALU.min))
                    dve.tensor_tensor(top1[:], pair_hi[:, :, 0], pair_hi[:, :, 1], ALU.max)
                    dve.tensor_tensor(low_hi[:], pair_hi[:, :, 0], pair_hi[:, :, 1], ALU.min)
                    link(dve.tensor_tensor(hi_lo[:], pair_lo[:, :, 0], pair_lo[:, :, 1], ALU.max))
                    link(dve.tensor_tensor(top2[:], low_hi[:], hi_lo[:], ALU.max))
                    link(dve.tensor_tensor(group_sum[:, :, 0:G], top1[:].rearrange("p (n g) -> p n g", g=G),
                                           top2[:].rearrange("p (n g) -> p n g", g=G), ALU.add))
                    dve.nop(nofuse=True)
                    for n in range(KB):
                        last = dve.max(group_top[:, n, :], group_sum[:, n, :])
                    link(last)
                    dve.nop(nofuse=True)
                    for n in range(KB):
                        last = dve.match_replace(group_left[:, n, :], group_top[:, n, :], group_sum[:, n, :], -BIG)
                    link(last)

                def choose_experts():
                    link(dve.tensor_scalar(group_mask[:], group_left[:, :, 0:G], -0.5 * BIG, None, ALU.is_le))
                    link(dve.tensor_tensor(masked[:].rearrange("p n (g j) -> p (n g) j", g=G),
                                           biased[:].rearrange("p n (g j) -> p (n g) j", g=G),
                                           group_mask[:].rearrange("p n g -> p (n g)").unsqueeze(2).broadcast_to(
                                               [P, KB * G, E // G]), ALU.mult))
                    dve.nop(nofuse=True)
                    for n in range(KB):
                        last = dve.max(expert_top[:, n, :], masked[:, n, :])
                    link(last)
                    dve.nop(nofuse=True)
                    for n in range(KB):
                        last = dve.match_replace(expert_left[:, n, :], expert_top[:, n, :], masked[:, n, :], -BIG)
                    link(last)
                    link(dve.tensor_scalar(chosen[:], expert_left[:], -0.5 * BIG, None, ALU.is_le))

                def weigh_experts():
                    link(dve.tensor_tensor(weight[:], score[:], chosen[:], ALU.mult))
                    link(dve.tensor_reduce(weight_sum[:], weight[:], AX_X, ALU.add))
                    link(dve.tensor_scalar(weight_sum[:], weight_sum[:], 1e-20, None, ALU.add))
                    link(dve.reciprocal(weight_sum[:], weight_sum[:]))
                    link(dve.tensor_tensor(combine[:], weight[:], weight_sum[:].unsqueeze(2).broadcast_to([P, KB, E]),
                                           ALU.mult))
                    link(dve.tensor_scalar(combine[:], combine[:], 2.5, None, ALU.mult))
                    link(dve.tensor_copy(combine_pc[:, :, 0, :], combine[:]))
                    link(dve.tensor_tensor(combine_rest[:], combine[:], combine_pc[:, :, 0, :], ALU.subtract))
                    link(dve.tensor_copy(combine_pc[:, :, 1, :], combine_rest[:]))
                    dve.tensor_tensor(combine_pc[:, :, 2, :], combine_rest[:], combine_pc[:, :, 1, :],
                                      ALU.subtract).then_inc(combine_done, 1)

                def gate_block(n):
                    e = (BLK + 1) * b + n
                    dve.wait_ge(silu_done, e + 1)
                    dve.wait_ge(up_mm, e + 1)
                    dve.tensor_tensor(gated[:, n % NGATED, :], bank[5], silu_g[:, n % 2, :],
                                      ALU.mult).then_inc(gated_done, 1)

                def weigh_block(n):
                    if n >= 2:
                        dve.wait_ge(down_mm, (BLK + 1) * b + n - 1)
                    dve.wait_ge(gated_done, (BLK + 1) * b + n + 1)
                    dve.wait_ge(spread_mm, BLK * b + n + 1)
                    dve.tensor_tensor(inner[:, n % 2, :], bank[6], gated[:, n % NGATED, :],
                                      ALU.mult).then_inc(inner_done, 1)

                def steps(h):
                    if h == DVE_AT["comb"]:
                        combine_heads()
                    if maxima_next and h == DVE_AT["hand"]:
                        hand_over(b + 1)
                    if h == DVE_AT["residual"]:
                        residual()
                        variance(link, x1, var2_done)
                    if h == DVE_AT["norm"]:
                        dve.wait_ge(rstd2_done, b + 1)
                        normalise(x1, h2_nat, h2_done)
                    if h == DVE_AT["split"]:
                        dve.wait_ge(h2_t_done, b + 1)
                        link(dve.tensor_copy(h2_hi[:], h2_t))
                        dve.tensor_tensor(h2_lo[:], h2_t, h2_hi[:], ALU.subtract).then_inc(h2_split, 1)
                    if h == DVE_AT["rank"]:
                        rank_groups()
                    if h == DVE_AT["choose"]:
                        choose_experts()
                    if h == DVE_AT["weigh"]:
                        weigh_experts()

                batch_columns(mod_post, 2, 5, b)
                dve.wait_ge(pv_done, ONE + NU * (b + 1))
                for c in range(2, 4):
                    dve.tensor_copy(ctx_t[:, c, :], bank[4 + c]).then_inc(ctx_copied_v, 1)
                for k in range(SLOTS):
                    steps(2 * k)
                    if maxima_next and 1 <= k <= NG:
                        group_halves(b + 1, k - 1)
                    steps(2 * k + 1)
                    if maxima_next and LAG <= k < NG + LAG:
                        group_reduce(b + 1, k - LAG)
                    if maxima_next and k == NG + LAG:
                        negate_maxima(b + 1)
                    if GATES <= k <= GATES + BLK:
                        gate_block(k - GATES)
                    for n in weighted_at[k]:
                        if n < BLK:
                            weigh_block(n)
                dve.wait_ge(y_turned, b + 1)
                dve.tensor_tensor(x1[:], bank[6].rearrange("p (n d) -> p n d", d=D), x1[:],
                                  ALU.add).then_inc(x2_done, 1)
                if count != OUT_LINKS:
                    raise ValueError(f"OUT_LINKS is {count}")

            prepare(0, first=True)
            dve.wait_ge(tables_in, 16 * len(table_loads))
            dve.tensor_copy(rel_lead[:], rel_lead32).then_inc(rel_lead_ready, 1)
            hand_over(0)
            for k in range(1, NG + LAG):
                if k <= NG:
                    group_halves(0, k - 1)
                if k >= LAG:
                    group_reduce(0, k - LAG)
            negate_maxima(0)
            cut_table()
            with dve.Fori(0, B - 1) as t:
                prepare(t + 1)
                after_attend(t, True)
            after_attend(B - 1, False)

        @block.tensor
        def _(pe):
            pe.wait_ge(silu_c_done, 1)
            for m in range(6):
                last = pe.matmul(ps[:, 0, B * m:B * (m + 1)], wmod[:, D * m:D * (m + 1)], silu_c, start=True, stop=True)
            last.then_inc(mod_mm, 1)

            def turn(dst, src, identity):
                for n in range(KB):
                    last = pe.transpose(dst(n), src(n), identity)
                return last

            def cut(tile, n):
                return tile[:, P * n:P * (n + 1)]

            def turn_h(b):
                pe.wait_ge(h_done, ONE + b + 1)
                turn(lambda n: cut(bank[3], n), lambda n: x_pre[:, n, :], ident[:]).then_inc(h_turned, 1)

            def project(b, w, before, done):
                pe.wait_ge(before, b + 1)
                pe.matmul(bank[3], w[:], h_t[:], start=True, stop=True).then_inc(done, 1)

            def project_v(b):
                pe.wait_ge(k_biased, b + 1)
                for n in range(KB):
                    last = pe.matmul(cut(bank[3], n), cut(h_t, n), wv[:], start=True, stop=True)
                last.then_inc(v_mm, 1)

            def linear_half(b, half):
                if half == 0:
                    pe.wait_ge(sigma_done, ONE + b + 1)
                    pe.nop(nofuse=True)
                    pe.wait_ge(v_new_done, b + 1)
                else:
                    pe.wait_ge(linear_halves, ONE + 2 * b + 1)
                for n in range(2):
                    last = pe.matmul(ps[:, 3, (D + H) * n:(D + H) * (n + 1)], cut(sigma, 2 * half + n), mz[:],
                                     start=True, stop=True)
                last.then_inc(linear_mm, 1)

            def lead_scores(b, g):
                pe.wait_ge(operands_a, ONE + 2 * NG * b + 2 * g + 2)
                for kb in range(KB):
                    n = KB * g + kb
                    dst = bank[n % NT]
                    if n >= NT:
                        pe.wait_ge(scores_copied, KB * NG * b + n - NT + 1)
                    else:
                        pe.wait_ge(exps, ONE + KB * NG * b)
                    keys = k_pc if near(kb, g) else far_pc
                    last = pe.matmul(dst, cut(keys[:, 0, :], kb), content_op[:, g % 2, :], start=True,
                                     stop=not near(kb, g), skip_group_check=True)
                    for u in range(2 if near(kb, g) else 0):
                        t0 = P * kb - (QG * g + H * u) + S - 1
                        last = pe.matmul(dst.rearrange("p (h q) -> p h q", q=QG)[:, :, H * u:H * (u + 1)],
                                         rel_lead[:, t0:t0 + P], rel_op[:, g % 2, 256 * u:256 * (u + 1)],
                                         start=False, stop=(u == 1), skip_group_check=True)
                    last.then_inc(scores_a, 1)

            def turn_maxima(b, g):
                if g == 0:
                    pe.wait_ge(linear_halves, ONE + 2 * (b + 1))
                else:
                    pe.wait_ge(group_maxima, NG * b + g)
                pe.wait_ge(key_maxima, NG * b + g + 1)
                turn(lambda c: cut(bank[3].bitcast(BF16), c), lambda c: cut(key_max[:, g % NCOPY, :], c),
                     identb[:]).then_inc(max_turned, 1)

            def turn_col_max(b):
                pe.wait_ge(group_maxima, NG * (b + 1))
                pe.nop(nofuse=True)
                pe.transpose(bank[3].bitcast(BF16)[0:KB * NG, 0:P], col_max[:].rearrange("p c g -> p (c g)"),
                             identb[:]).then_inc(col_max_turned, 1)

            def full_scores(b, n):
                kb, g = n // NG, n % NG
                dst = bank[n % NT]
                if n >= NT:
                    pe.wait_ge(exps, ONE + KB * NG * b + n - NT + 1)
                keys = kst if near(kb, g) else kst_far
                for hp in range(HP):
                    last = pe.matmul(dst[:, 2 * QG * hp:2 * QG * (hp + 1)], cut(keys[:, hp, :], kb),
                                     qst[:, hp, :, QG * g:QG * (g + 1)], start=(hp == 0),
                                     stop=(hp == HP - 1 and not near(kb, g)), skip_group_check=True)
                by_query = dst.rearrange("p (h q) -> p h q", q=QG)
                for j in range(0, QG if near(kb, g) else 0, 2):
                    q0 = QG * g + j
                    t0 = P * kb - q0 + S - 1
                    last = pe.matmul(by_query[:, :, j:j + 2], rel[:, t0:t0 + P], qrel[:, :, q0:q0 + 2],
                                     start=False, stop=(j == QG - 2), skip_group_check=True)
                last.then_inc(scores_b, 1)

            def values(b, u, quarters):
                kb, half = u // 2, u % 2
                if u == 0 and 0 in quarters:
                    pe.wait_ge(handed_over, ONE + 2 * b + 2)
                    pe.nop(nofuse=True)
                    pe.wait_ge(x2_done, ONE + b)
                    pe.nop(nofuse=True)
                pe.wait_ge(exps, ONE + KB * NG * b + UNIT * (u + 1))
                for c in quarters:
                    for j in range(4):
                        last = pe.matmul(ps[32 * j:32 * (j + 1), 4 + c, QU * half:QU * (half + 1)],
                                         v_ones[:, kb, 4 * c + j, :], probs[:, u % 2, 4 * c + j, :],
                                         start=(u == 0), stop=(kb == KB - 1), tile_position=(0, 32 * j),
                                         skip_group_check=True)
                if 3 in quarters:
                    last.then_inc(pv_done, 1)

            def attend(b, prepare_next):
                pe.wait_ge(stacks_in, ONE + 16 * N_STACK * (b + 1))
                pe.nop(nofuse=True)
                pe.wait_ge(max_in, ONE + 16 * N_MAX * (b + 1))
                for n in range(KB * NG):
                    full_scores(b, n)
                    if n >= UNIT and n % UNIT in VALUES:
                        values(b, n // UNIT - 1, [VALUES.index(n % UNIT)])
                    if prepare_next and n == TURN_H:
                        turn_h(b + 1)
                    if prepare_next and n == MM_Q:
                        project(b + 1, wq, h_t_done, q_mm)
                    if prepare_next and n == MM_K:
                        project(b + 1, wk, q_biased, k_mm)
                    if prepare_next and n == MM_V:
                        project_v(b + 1)
                    if prepare_next and n == MM_LIN0:
                        linear_half(b + 1, 0)
                    if prepare_next and n == MM_LIN1:
                        linear_half(b + 1, 1)
                values(b, NU - 1, range(4))

            def after_attend(b, maxima_next):
                def two_part_product(dst, w_hi, w_lo):
                    pe.matmul(dst, w_lo, h2_hi[:], start=True, stop=False)
                    pe.matmul(dst, w_hi, h2_lo[:], start=False, stop=False)
                    return pe.matmul(dst, w_hi, h2_hi[:], start=False, stop=True)

                def down(n):
                    if n < BLK:
                        pe.wait_ge(inner_done, BLK * b + n + 1)
                        src = inner[:, n % 2, :]
                    else:
                        pe.wait_ge(gated_done, (BLK + 1) * (b + 1))
                        src = gated[:, n % NGATED, :]
                    pe.matmul(bank[7], wd[:, n, :], src, start=(n == 0), stop=(n == BLK - 1)).then_inc(down_mm, 1)

                def steps(h):
                    if h == PE_AT["context"]:
                        pe.wait_ge(ctx_copied_a, 2 * b + 2)
                        pe.wait_ge(ctx_copied_v, 2 * b + 2)
                        for n in range(KB):
                            for c in range(4):
                                last = pe.transpose(cut(bank[4 + n], c), cut(ctx_t[:, c, :], n), ident[:])
                        last.then_inc(ctx_turned, 1)
                    if h == PE_AT["comb"]:
                        pe.wait_ge(comb_done, ONE + b + 1)
                        turn(lambda n: cut(bank[4], n), lambda n: comb[:, n, :], ident[:]).then_inc(comb_turned, 1)
                    if h == PE_AT["attn"]:
                        pe.wait_ge(comb_t_done, b + 1)
                        pe.matmul(bank[5], wo[:], comb_t, start=True, stop=True).then_inc(attn_mm, 1)
                    if h == PE_AT["attn_turn"]:
                        pe.wait_ge(attn_t_done, b + 1)
                        turn(lambda n: cut(bank[5], n), lambda n: cut(attn_t, n), ident[:]).then_inc(attn_turned, 1)
                    if h == PE_AT["h2"]:
                        pe.wait_ge(h2_done, b + 1)
                        turn(lambda n: cut(bank[6], n), lambda n: h2_nat[:, n, :], ident[:]).then_inc(h2_turned, 1)
                    if h == PE_AT["route"]:
                        pe.wait_ge(h2_t_done, b + 1)
                        for n in range(KB):
                            last = pe.matmul(ps[:, 7, E * n:E * (n + 1)], cut(h2_t, n), w_router[:],
                                             start=True, stop=True)
                        last.then_inc(logits_done, 1)
                    if h == PE_AT["weights"]:
                        pe.wait_ge(combine_done, b + 1)
                        turn(lambda n: bank[6].bitcast(BF16)[0:3 * E, P * n:P * (n + 1)],
                             lambda n: combine_pc[:, n, :, :].rearrange("p s e -> p (s e)"),
                             identb[:]).then_inc(combine_turned, 1)

                for k in range(SLOTS):
                    steps(2 * k)
                    if maxima_next and k < NG:
                        lead_scores(b + 1, k)
                    steps(2 * k + 1)
                    if maxima_next and LAG <= k < NG + LAG:
                        turn_maxima(b + 1, k - LAG)
                    if maxima_next and k == NG + LAG:
                        turn_col_max(b + 1)
                    if GATES <= k <= GATES + BLK:
                        n = k - GATES
                        if n >= 1:
                            pe.wait_ge(silu_done, (BLK + 1) * b + n)
                        else:
                            pe.wait_ge(h2_split, b + 1)
                        two_part_product(bank[4], wg_hi[:, n, :], wg_lo[:, n, :]).then_inc(gate_mm, 1)
                        if n >= 1:
                            pe.wait_ge(gated_done, (BLK + 1) * b + n)
                        two_part_product(bank[5], wu_hi[:, n, :], wu_lo[:, n, :]).then_inc(up_mm, 1)
                    for n in weighted_at[k]:
                        if n < BLK:
                            if n == 0:
                                pe.wait_ge(combine_t_done, b + 1)
                            else:
                                pe.wait_ge(inner_done, BLK * b + n)
                            pe.matmul(bank[6], sel[:, 2 * n:2 * n + 2, :].rearrange("p e i -> p (e i)"), combine_t,
                                      start=True, stop=True).then_inc(spread_mm, 1)
                        if 1 <= n < BLK:
                            down(n - 1)
                down(BLK)
                down(BLK - 1)
                pe.wait_ge(y_t_done, b + 1)
                turn(lambda n: cut(bank[6], n), lambda n: cut(y_t, n), ident[:]).then_inc(y_turned, 1)

            pe.wait_ge(first_in, 16 * len(first_loads))
            turn_h(0)
            project(0, wq, h_t_done, q_mm)
            project(0, wk, q_biased, k_mm)
            project_v(0)
            linear_half(0, 0)
            linear_half(0, 1)
            pe.wait_ge(masks_ready, 2)
            pe.wait_ge(rel_lead_ready, 1)
            for k in range(NG + LAG):
                if k < NG:
                    lead_scores(0, k)
                if k >= LAG:
                    turn_maxima(0, k - LAG)
            turn_col_max(0)
            pe.wait_ge(consts_ready, 4)
            pe.wait_ge(vec_set, VEC_SETS)
            pe.wait_ge(tables_in, 16 * len(table_loads))
            pe.wait_ge(experts_in, 16 * len(expert_loads))
            with pe.Fori(0, B - 1) as t:
                attend(t, True)
                after_attend(t, True)
            attend(B - 1, False)
            after_attend(B - 1, False)


def _layouts(v):
    f = np.float32
    t = lambda w: np.ascontiguousarray(np.asarray(w).T)
    by_dim = lambda w: np.asarray(w).reshape(H, HD, -1).transpose(1, 0, 2).reshape(D, -1)
    keys_of = np.clip(np.arange(2)[:, None] - (np.arange(TW) - (S - 1))[None, :], -MAX_REL, MAX_REL) + MAX_REL
    table = np.asarray(v["L0_attn_rel_emb"])[keys_of]
    rel = np.zeros((2, SLOT, TW), f)
    for r in range(len(PIECES)):
        rel[:, HD * r:HD * (r + 1)] = table.transpose(0, 2, 1)
    piece_mask = np.zeros((2, SLOT, 3), f)
    for r, (_, pk) in enumerate(PIECES):
        piece_mask[:, HD * r:HD * (r + 1), pk] = 1.0
    rel_lead = np.asarray(v["L0_attn_rel_emb"])[
        np.clip(np.arange(H)[:, None] - (np.arange(TW) - (S - 1))[None, :], -MAX_REL, MAX_REL) + MAX_REL]
    rel_far = np.stack([np.repeat(np.asarray(v["L0_attn_rel_emb"])[r], H) for r in (2 * MAX_REL, 0)], 1)
    mz = np.zeros((P, D + H), f)
    for h in range(H):
        mz[h::H, HD * h:HD * (h + 1)] = np.asarray(v["L0_attn_M"])[h]
        mz[h::H, D + h] = np.asarray(v["L0_attn_z"])[h]

    def inner_weights(routed, shared):
        w = np.concatenate([np.asarray(routed).reshape(E * I, D), np.asarray(shared)], 0)
        return np.ascontiguousarray(w.T).reshape(D, BLK + 1, P)

    down = np.asarray(v["L0_ffn_w_down"]).transpose(0, 2, 1).reshape(BLK, P, D)
    down = np.concatenate([down, t(v["L0_ffn_sh_down"])[None]], 0).transpose(1, 0, 2)
    return {
        "x": np.asarray(v["L0_attn_hidden_states"]), "c": t(v["L0_c"]),
        "rel_lead": np.ascontiguousarray(rel_lead.transpose(2, 0, 1)).reshape(P, TW), "rel_far": rel_far,
        "own": np.tile(np.eye(H, dtype=f), (HD, 1)),
        "ident": np.eye(P, dtype=f), "wq": t(by_dim(v["L0_attn_Wq"])), "wk": t(by_dim(v["L0_attn_Wk"])),
        "wv": t(v["L0_attn_Wv"]), "wo": t(v["L0_attn_Wo"]),
        "bq": by_dim(v["L0_attn_bq"]).reshape(P, 1), "bk": by_dim(v["L0_attn_bk"]).reshape(P, 1),
        "bv": np.asarray(v["L0_attn_bv"]), "bo": np.asarray(v["L0_attn_bo"]).reshape(P, 1),
        "wmod": np.asarray(v["L0_wmod"]), "mz": mz,
        "gate_alpha": np.asarray(v["L0_attn_gate_alpha"]).reshape(1), "rel": rel.reshape(P, TW),
        "piece_mask": piece_mask.reshape(P, 3), "w_router": t(v["L0_ffn_gate_w"]),
        "b_router": np.asarray(v["L0_ffn_gate_bias"]),
        "wg": inner_weights(v["L0_ffn_w_gate"], v["L0_ffn_sh_gate"]),
        "wu": inner_weights(v["L0_ffn_w_up"], v["L0_ffn_sh_up"]),
        "wd": np.ascontiguousarray(down),
        "sel": np.tile(np.eye(E, dtype=f), (3, 1)),
    }


def kernel(**inputs):
    import concourse.bacc as bacc
    from concourse.bass_utils import run_bass_kernel_spmd

    nc = bacc.Bacc("TRN2", target_bir_lowering=False, num_devices=1)
    arrays, aps = {}, {}
    for name, value in _layouts(inputs).items():
        value = np.ascontiguousarray(value)
        arrays[f"in_{name}"] = value
        aps[name] = nc.dram_tensor(f"in_{name}", value.shape, mybir.dt.from_np(value.dtype),
                                   kind="ExternalInput").ap()
    out = nc.dram_tensor("out", (B, S, D), F32, kind="ExternalOutput").ap()
    build(nc, aps, out)
    result = run_bass_kernel_spmd(nc, [arrays], core_ids=[0])
    return result.results[0]["out"]
```
